# Optimizing a Trainium2 kernel written in Bass

```python
import numpy as np
import jax
import jax.numpy as jnp

def _softmax(x, axis=-1):
    return jax.nn.softmax(x, axis=axis)

def _gelu(x):
    return jax.nn.gelu(x, approximate=True)

def _silu(x):
    return jax.nn.silu(x)

def _sigmoid(x):
    return jax.nn.sigmoid(x)

def _layernorm(x, axis=-1, eps=1e-05):
    m = jnp.mean(x, axis=axis, keepdims=True)
    v = jnp.var(x, axis=axis, keepdims=True)
    return (x - m) / jnp.sqrt(v + eps)

def _scatter_add(tgt, idx, src, axis=0):
    return tgt.at[idx].add(src)

def _segment_sum(src, seg, n):
    return jax.ops.segment_sum(src, seg, n)
kernel_name = 'mk_xattn_ffn_d1_seqx_r4_4554ca'

def setup_inputs(seed: int=0):
    np.random.seed(seed)
    _w = jnp.asarray

    def _rec_inputs():
        import jax
        import jax.numpy as jnp
        _rk = jax.random.key(seed)
        x = -0.0003929 + 0.9999 * jax.random.normal(jax.random.fold_in(_rk, 1), (8, 256, 1024), jnp.float32)
        _lenS = 256 - jax.random.randint(jax.random.fold_in(_rk, 7), (8,), 0, max(1, 256 // 4) + 1, jnp.int32)
        _lenS2 = 256 - jax.random.randint(jax.random.fold_in(_rk, 8), (8,), 0, max(1, 256 // 4) + 1, jnp.int32)
        _ctx_4096P = jax.random.normal(jax.random.fold_in(_rk, 11), (8, 16, 1024), jnp.float32)
        _ctx_4096c = jax.random.dirichlet(jax.random.fold_in(_rk, 511), 0.3 * jnp.ones((16,), jnp.float32), (8, 256))
        _ctx_4096t = jnp.einsum('bsk,bkd->bsd', _ctx_4096c, _ctx_4096P)
        _ctx_4096t = _ctx_4096t * jax.lax.rsqrt(jnp.mean(jnp.square(_ctx_4096t)) + 1e-12) * 0.953939
        ctx_4096 = 2.81802e-05 + 1.00001 * (_ctx_4096t + 0.3 * jax.random.normal(jax.random.fold_in(_rk, 611), (8, 256, 1024), jnp.float32))
        pos_BxS2 = jnp.broadcast_to(jnp.arange(256, dtype=jnp.int32), (8, 256))
        _validS = jnp.arange(256)[None, :] < _lenS[:, None]
        _validS2 = jnp.arange(256)[None, :] < _lenS2[:, None]
        _causal = jnp.tril(jnp.ones((256, 256), dtype=bool))
        mask_BxSxS2_ik0 = jnp.where(jnp.broadcast_to(_validS2[:, None, :], (8, 256, 256)), 0, 1).astype(jnp.int32)
        return (x, ctx_4096, pos_BxS2, mask_BxSxS2_ik0)
    x, ctx_4096, pos_BxS2, mask_BxSxS2_ik0 = _rec_inputs()

    def _L0_xattn_setup():
        import jax, jax.numpy as jnp
        import numpy as np
        B, S, E = (2, 512, 1024)
        H, KVH, D = (32, 8, 128)
        GROUPS = H // KVH
        MAX_POS = 1024
        ROPE_THETA = 10000.0

        def _rope_tables(max_pos, dim, theta):
            inv_freq = 1.0 / theta ** (jnp.arange(0, dim, 2, dtype=jnp.float32) / dim)
            t = jnp.arange(max_pos, dtype=jnp.float32)
            freqs = jnp.einsum('i,j->ij', t, inv_freq)
            emb = jnp.concatenate([freqs, freqs], axis=-1)
            return (jnp.cos(emb), jnp.sin(emb))

        def _rotate_half(x):
            x1, x2 = (x[..., :x.shape[-1] // 2], x[..., x.shape[-1] // 2:])
            return jnp.concatenate([-x2, x1], axis=-1)
        key = jax.random.key(seed)
        ks = jax.random.split(key, 8)
        scale_w = 1.0 / np.sqrt(E)
        query = jax.random.normal(ks[0], (B, S, E), dtype=jnp.float32)
        k_in = jax.random.normal(ks[1], (B, S, E), dtype=jnp.float32)
        v_in = jax.random.normal(ks[2], (B, S, E), dtype=jnp.float32)
        position_ids = jnp.broadcast_to(jnp.arange(S, dtype=jnp.int64), (B, S))
        src_mask = jnp.tril(jnp.ones((S, S), dtype=jnp.int32))
        src_mask = jnp.broadcast_to(src_mask, (B, S, S))
        Wq = jax.random.normal(ks[3], (E, H * D), dtype=jnp.float32) * scale_w
        Wk = jax.random.normal(ks[4], (E, KVH * D), dtype=jnp.float32) * scale_w
        Wv = jax.random.normal(ks[5], (E, KVH * D), dtype=jnp.float32) * scale_w
        Wo = jax.random.normal(ks[6], (H * D, E), dtype=jnp.float32) * scale_w
        return {'query': query, 'key': k_in, 'value': v_in, 'position_ids': position_ids, 'src_mask': src_mask, 'Wq': Wq, 'Wk': Wk, 'Wv': Wv, 'Wo': Wo}
    _L0_xattn_all = _L0_xattn_setup()
    _L0_xattn_in = {k: v for k, v in _L0_xattn_all.items() if k in ('Wq', 'Wk', 'Wv', 'Wo')}
    del _L0_xattn_all

    def _L0_ffn_setup():
        import jax, jax.numpy as jnp
        import numpy as np
        BITS = 4
        GROUP_SIZE = 128
        IN_FEATURES = 1024
        OUT_FEATURES = 1024
        MAXQ = 2 ** BITS - 1
        PACK = 32 // BITS

        def _dequantize(qweight, qzeros, scales):
            shifts = jnp.arange(0, 32, BITS, dtype=jnp.int32)
            zeros = qzeros[:, :, None] >> shifts[None, None, :] & MAXQ
            zeros = zeros.reshape(scales.shape).astype(scales.dtype)
            w = qweight[:, None, :] >> shifts[None, :, None] & MAXQ
            w = w.reshape(-1, qweight.shape[-1]).astype(scales.dtype)
            scales_full = jnp.repeat(scales, GROUP_SIZE, axis=0)
            zeros_full = jnp.repeat(zeros, GROUP_SIZE, axis=0)
            return scales_full * (w - zeros_full)
        key = jax.random.key(seed)
        k = jax.random.split(key, 5)
        x = jax.random.normal(k[0], (8, 512, IN_FEATURES), dtype=jnp.float32)
        qweight = jax.random.randint(k[1], (IN_FEATURES // PACK, OUT_FEATURES), 0, 2 ** 31 - 1, dtype=jnp.int32)
        n_groups = IN_FEATURES // GROUP_SIZE
        qzeros = jax.random.randint(k[2], (n_groups, OUT_FEATURES // PACK), 0, 2 ** 31 - 1, dtype=jnp.int32)
        scales = jax.random.uniform(k[3], (n_groups, OUT_FEATURES), dtype=jnp.float32) * 0.01 + 0.001
        bias = jax.random.normal(k[4], (OUT_FEATURES,), dtype=jnp.float32) * 0.01
        return {'x': x, 'qweight': qweight, 'qzeros': qzeros, 'scales': scales, 'bias': bias}
    _L0_ffn_all = _L0_ffn_setup()
    _L0_ffn_in = {k: v for k, v in _L0_ffn_all.items() if k in ('qweight', 'qzeros', 'scales', 'bias')}
    del _L0_ffn_all
    return {'x': x, 'ctx_4096': ctx_4096, 'pos_BxS2': pos_BxS2, 'mask_BxSxS2_ik0': mask_BxSxS2_ik0, 'L0_xattn_Wq': _L0_xattn_in['Wq'], 'L0_xattn_Wk': _L0_xattn_in['Wk'], 'L0_xattn_Wv': _L0_xattn_in['Wv'], 'L0_xattn_Wo': _L0_xattn_in['Wo'], 'L0_ffn_qweight': _L0_ffn_in['qweight'], 'L0_ffn_qzeros': _L0_ffn_in['qzeros'], 'L0_ffn_scales': _L0_ffn_in['scales'], 'L0_ffn_bias': _L0_ffn_in['bias']}

def reference(x, ctx_4096, pos_BxS2, mask_BxSxS2_ik0, L0_xattn_Wq, L0_xattn_Wk, L0_xattn_Wv, L0_xattn_Wo, L0_ffn_qweight, L0_ffn_qzeros, L0_ffn_scales, L0_ffn_bias):
    import jax
    import jax.numpy as jnp

    def _L0_xattn_ref(query, key, value, position_ids, src_mask, Wq, Wk, Wv, Wo):
        import jax, jax.numpy as jnp
        import numpy as np
        B, S, E = (2, 512, 1024)
        H, KVH, D = (32, 8, 128)
        GROUPS = H // KVH
        MAX_POS = 1024
        ROPE_THETA = 10000.0

        def _rope_tables(max_pos, dim, theta):
            inv_freq = 1.0 / theta ** (jnp.arange(0, dim, 2, dtype=jnp.float32) / dim)
            t = jnp.arange(max_pos, dtype=jnp.float32)
            freqs = jnp.einsum('i,j->ij', t, inv_freq)
            emb = jnp.concatenate([freqs, freqs], axis=-1)
            return (jnp.cos(emb), jnp.sin(emb))

        def _rotate_half(x):
            x1, x2 = (x[..., :x.shape[-1] // 2], x[..., x.shape[-1] // 2:])
            return jnp.concatenate([-x2, x1], axis=-1)
        nb, q_len, _ = query.shape
        q = (query @ Wq).reshape(nb, q_len, H, D).transpose(0, 2, 1, 3)
        k = (key @ Wk).reshape(nb, q_len, KVH, D).transpose(0, 2, 1, 3)
        v = (value @ Wv).reshape(nb, q_len, KVH, D).transpose(0, 2, 1, 3)
        cos_t, sin_t = _rope_tables(MAX_POS, D, ROPE_THETA)
        cos = cos_t[position_ids][:, None]
        sin = sin_t[position_ids][:, None]
        q = q * cos + _rotate_half(q) * sin
        k = k * cos + _rotate_half(k) * sin
        k = jnp.repeat(k, GROUPS, axis=1)
        v = jnp.repeat(v, GROUPS, axis=1)
        scores = jnp.einsum('bhqd,bhkd->bhqk', q, k) / jnp.sqrt(jnp.float32(D))
        mask = src_mask[:, None]
        scores = jnp.where(mask == 0, jnp.float32(-1000000000.0), scores)
        attn = jax.nn.softmax(scores, axis=-1)
        x = jnp.einsum('bhqk,bhkd->bhqd', attn, v)
        x = x.transpose(0, 2, 1, 3).reshape(nb, q_len, H * D)
        return x @ Wo

    def _L0_ffn_ref(x, qweight, qzeros, scales, bias):
        import jax, jax.numpy as jnp
        import numpy as np
        BITS = 4
        GROUP_SIZE = 128
        IN_FEATURES = 1024
        OUT_FEATURES = 1024
        MAXQ = 2 ** BITS - 1
        PACK = 32 // BITS

        def _dequantize(qweight, qzeros, scales):
            shifts = jnp.arange(0, 32, BITS, dtype=jnp.int32)
            zeros = qzeros[:, :, None] >> shifts[None, None, :] & MAXQ
            zeros = zeros.reshape(scales.shape).astype(scales.dtype)
            w = qweight[:, None, :] >> shifts[None, :, None] & MAXQ
            w = w.reshape(-1, qweight.shape[-1]).astype(scales.dtype)
            scales_full = jnp.repeat(scales, GROUP_SIZE, axis=0)
            zeros_full = jnp.repeat(zeros, GROUP_SIZE, axis=0)
            return scales_full * (w - zeros_full)
        out_shape = x.shape[:-1] + (OUT_FEATURES,)
        x2d = x.reshape(-1, x.shape[-1])
        W = _dequantize(qweight, qzeros, scales)
        out = jnp.matmul(x2d, W) + bias
        return out.reshape(out_shape)
    x = x + _L0_xattn_ref(_layernorm(x, axis=-1), ctx_4096, ctx_4096, pos_BxS2, mask_BxSxS2_ik0, L0_xattn_Wq, L0_xattn_Wk, L0_xattn_Wv, L0_xattn_Wo)
    x = x + _L0_ffn_ref(_layernorm(x, axis=-1), L0_ffn_qweight, L0_ffn_qzeros, L0_ffn_scales, L0_ffn_bias)
    return x

_drawn_inputs = setup_inputs


def setup_inputs(seed=0):
    import zlib

    import numpy as np

    out = dict(_drawn_inputs(seed))
    spreads = {}
    factors = {'L0_ffn_bias': 8.0}
    for name, (base, spread) in spreads.items():
        noise = np.random.default_rng([zlib.crc32(name.encode()), seed]).standard_normal(out[name].shape)
        drawn = base * np.exp(spread * noise) if base else spread * noise
        out[name] = jnp.asarray(drawn.astype(out[name].dtype))
    for name, factor in factors.items():
        out[name] = (out[name] * factor).astype(out[name].dtype)
    return out
```

```python
from contextlib import ExitStack

import numpy as np

import concourse.bass as bass
from concourse import mybir

ALU = mybir.AluOpType
ACT = mybir.ActivationFunctionType
F32 = mybir.dt.float32
F32R = mybir.dt.float32r
I32 = mybir.dt.int32
U8 = mybir.dt.uint8
AX = mybir.AxisListType

P = 128
E = 1024
KT = E // P
B, S = 8, 256
H, KVH, D = 32, 8, 128
HD2 = D // 2
HALVES = 2
HB = B // HALVES
T = HB * S
TT = T // P
CH = 2
CB = HB // CH
CT = T // CH
NW = 512
NH = E // NW
PAIRS = H // 2
PU = 4
UNITS = PAIRS * PU
MAX_POS, THETA = 1024, 10000.0
SCALE = float(np.float32(1.0) / np.sqrt(np.float32(D)))
MASKED = float(np.float32(-1e9) * np.sqrt(np.float32(D)))
EPS = 1e-5
BITS = 4
NIB = 32 // BITS
GS = 128
RAW_V = 4
RAW_A = 2 * RAW_V + KVH
RAW_B0 = RAW_A + 2
RAW_C0 = RAW_A + PAIRS * PU
RAWS = RAW_C0 + 2
KVU = 2 * TT + 2 * KVH
K0 = TT
V1 = TT + 2 * KVH
TR_CS, TR_X = 2 * TT, 2 * TT + TT // 2
TR_X2 = TR_X + 2 * TT
TRS = TR_X2 + 2 * TT
WOS = TT * NH
BK_S, BK_Q, BK_T, BK_O, BK_W = 0, 2, 3, 5, 6


def rope_table():
    steps = np.arange(0, D, 2, dtype=np.float32) / np.float32(D)
    inv_freq = np.float32(1) / np.power(THETA, steps.astype(np.float64)).astype(np.float32)
    freqs = np.arange(MAX_POS, dtype=np.float32)[:, None] * inv_freq[None]
    cos = np.cos(freqs.astype(np.float64)).astype(np.float32)
    sin = np.sin(freqs.astype(np.float64)).astype(np.float32)
    return np.concatenate([cos, cos, sin, -sin], axis=1)


def build(nc, x, ctx4, pos, mask, wq, wk, wv, wo, qweight, qzeros, scales, bias, table, ident, out):
    x_rows = x.rearrange("b s e -> (b s) e").rearrange("(h t p) e -> h t p e", p=P, t=TT)
    c_rows = ctx4.rearrange("b s e -> (b s) e").rearrange("(h t p) e -> h t p e", p=P, t=TT)
    o_rows = out.rearrange("b s e -> (b s) e").rearrange("(h t p) e -> h t p e", p=P, t=TT)
    pos_cols = pos.rearrange("b s -> (b s)").rearrange("(h t p) -> h p t", p=P, t=TT)
    mask_rows = mask.rearrange("(h b) (q p) k -> h p b q k", p=P, b=HB)
    wq_heads = wq.rearrange("(k p) (h d) -> h p k d", p=P, d=D)
    wk_heads = wk.rearrange("(k p) (h d) -> h p k d", p=P, d=D)
    wv_blocks = wv.rearrange("(a k p) (n c) -> n a p k c", p=P, k=KT // RAW_V, c=NW)
    wo_blocks = wo.rearrange("(j t p) (n c) -> j n p t c", p=P, t=2, c=NW)

    with ExitStack() as stack:
        def sb(name, shape, dt):
            return stack.enter_context(nc.sbuf_tensor(name, shape, dt))

        def sem(name):
            return stack.enter_context(nc.semaphore(name))

        def fori(eng, *span):
            return eng.Fori(*span)

        act_t = sb("act_t", [P, 2 * KT * T], F32R)
        parts = sb("parts", [P, 16384], F32R)
        rows = sb("rows", [P, TT, E], F32)
        raw = [sb(f"raw{i}", [P, E], F32) for i in range(2)]
        q_parts = sb("q_parts", [P, 2, CT], F32R)
        rope_cos = sb("rope_cos", [P, T], F32)
        rope_sin = sb("rope_sin", [P, T], F32)
        scores = sb("scores", [P, HB * 2 * S], F32)
        mask8 = sb("mask8", [P, HB * 2, S], U8)
        probs = sb("probs", [P, CB * 2 * S], F32)
        probs_t = sb("probs_t", [P, CB, 2, 2, S], F32R)
        rope_tmp = sb("rope_tmp", [P, 2, NW], F32)
        identity = sb("identity", [P, P], F32)
        idx = sb("idx", [P, TT], I32)
        idx_neg = sb("idx_neg", [P, TT], I32)
        zero_words = sb("zero_words", [P, E // NIB], I32)
        stats = sb("stats", [P, TT, NH, 6], F32)
        mean_var = sb("mean_var", [P, TT, 2], F32)
        ln_tmp = sb("ln_tmp", [P, 4, TT], F32)
        inv_std = sb("inv_std", [P, TT], F32)
        row_max = sb("row_max", [P, 4], F32)
        neg_max = sb("neg_max", [P, 4], F32)
        row_sum = sb("row_sum", [P, 4], F32)
        inv_sum = sb("inv_sum", [P, 4], F32)
        ps = stack.enter_context(nc.psum_tensor("ps", [P, 8, NW], F32))
        k_dram = nc.dram_tensor("k_scratch", [KVH, P, 2, T], F32, kind="Internal").ap()
        v_dram = nc.dram_tensor("v_scratch", [KVH, P, TT, 2, D], F32, kind="Internal").ap()

        act_v = act_t[:, :].rearrange("p (l k t) -> p l k t", l=2, k=KT)
        o_parts = parts[:, 0:4096].rearrange("p (c j l t) -> p c j l t", c=CH, j=2, l=2)
        wo_parts = parts[:, 4096:8192].rearrange("p (n j l c) -> p n j l c", n=NH, j=2, l=2)
        wq_parts = parts[:, 8192:12288].rearrange("p (s k l d) -> p s k l d", s=2, k=KT, l=2)
        kv_parts = parts[:, 12288:16384]
        k_parts = [kv_parts[:, c * 2048:c * 2048 + 1024].rearrange("p (l t) -> p l t", l=2) for c in range(CH)]
        v_parts = [kv_parts[:, c * 2048 + 1024:c * 2048 + 2048].rearrange("p (t l d) -> p t l d", l=2, d=D)
                   for c in range(CH)]
        kv_out = [kv_parts[:, s * 1024:(s + 1) * 1024].rearrange("p (l t) -> p l t", l=2) for s in range(4)]
        wv_parts = parts[:, 0:8192].rearrange("p (k l c) -> p k l c", k=KT, l=2)
        w_parts = [parts[:, 8192:16384].rearrange("p (k l c) -> p k l c", k=KT, l=2), wv_parts]
        score_v = scores[:, :].rearrange("p (b q k) -> p b q k", b=HB, q=2)
        score_i = scores[:, :].bitcast(I32).rearrange("p (b q k) -> p b q k", b=HB, q=2)
        mask_v = mask8[:, :, :].rearrange("p (b q) k -> p b q k", b=HB)
        gathered = scores[:, :].rearrange("p (t c) -> p t c", t=TT)
        probs_v = probs[:, :].rearrange("p (b q k) -> p b q k", b=CB, q=2)
        normed = [probs[:, :], rope_tmp[:, :, :].rearrange("p a n -> p (a n)")]
        zeros_i = scores[:, 0:E].bitcast(I32)
        w_int = scores[:, E:E + NW].bitcast(I32)
        w_f32 = scores[:, E + NW:E + 2 * NW]
        bias_rows = rope_cos[:, 0:E]
        raw_i = [r[:, :].bitcast(I32) for r in raw]

        ident_in, zero_words_in = sem("ident_in"), sem("zero_words_in")
        half_open = sem("half_open")
        held = sem("held")
        pos_in, mask_in, bias_in = sem("pos_in"), sem("mask_in"), sem("bias_in")
        ctx_in = [sem(f"ctx_in{t}") for t in range(TT)]
        x_in = [sem(f"x_in{t}") for t in range(TT)]
        raw_in = [sem(f"raw_in{i}") for i in range(2)]
        table_in = sem("table_in")
        kv_stored = [sem(f"kv_stored{s}") for s in range(4)]
        k_in = [sem(f"k_in{c}") for c in range(CH)]
        v_in = [sem(f"v_in{c}") for c in range(CH)]
        out_stored = [sem(f"out_stored{t}") for t in range(TT)]
        raw_hi, raw_split = sem("raw_hi"), sem("raw_split")
        tr_done, tr_first, tr_second = sem("tr_done"), sem("tr_first"), sem("tr_second")
        idx_ready, idx_step = sem("idx_ready"), sem("idx_step")
        mask_ready, fill_done = sem("mask_ready"), sem("fill_done")
        kv_done, kv_hi, kv_lo = sem("kv_done"), sem("kv_hi"), sem("kv_lo")
        k_rot, k_sum = sem("k_rot"), sem("k_sum")
        ln_chain, ln_var, ln_root, ln_rows = sem("ln_chain"), sem("ln_var"), sem("ln_root"), sem("ln_rows")
        q_done, q_rot, q_sum, q_hi, q_lo = sem("q_done"), sem("q_rot"), sem("q_sum"), sem("q_hi"), sem("q_lo")
        s_done, s_masked, max_done, max_ready = sem("s_done"), sem("s_masked"), sem("max_done"), sem("max_ready")
        exp_done, inv_ready, p_ready = sem("exp_done"), sem("inv_ready"), sem("p_ready")
        pt_done, pt_hi, pt_lo = sem("pt_done"), sem("pt_hi"), sem("pt_lo")
        ot_done, ot_hi, ot_lo = sem("ot_done"), sem("ot_hi"), sem("ot_lo")
        wo_done, wo_added = sem("wo_done"), sem("wo_added")
        z_step, biased = sem("z_step"), sem("biased")
        w_step, w_full, w_hi, w_lo = sem("w_step"), sem("w_full"), sem("w_hi"), sem("w_lo")
        ffn_done, ffn_added = sem("ffn_done"), sem("ffn_added")

        block = stack.enter_context(nc.Block())

        def hold(eng):
            eng.sem_inc(held, 1)

        def products(eng, dst, left, right, n):
            for k in range(n):
                lh, ll = left(k)
                rh, rl = right(k)
                eng.matmul(dst, lh, rh, start=(k == 0), stop=False)
                eng.matmul(dst, lh, rl, start=False, stop=False)
                last = eng.matmul(dst, ll, rh, start=False, stop=(k == n - 1))
            return last

        @block.sync
        def _(sp):
            sp.dma_start(identity[:, :], ident).then_inc(ident_in, 16)
            sp.dma_start(zero_words[:, :],
                         qzeros.rearrange("g (a w) -> g a w", a=1).broadcast_to([KT, P // KT, E // NIB])
                         ).then_inc(zero_words_in, 16)
            for t in range(TT):
                sp.sem_inc(out_stored[t], 16)
            sp.sem_inc(raw_split, 1)
            sp.sem_inc(half_open, 1)
            with fori(sp, 0, HALVES) as hf:
                def load_raw(i, src):
                    sp.wait_ge(raw_split, hf * RAWS + 1 + max(i - 1, 0))
                    dst = raw_i[i % 2] if src.dtype == I32 else raw[i % 2][:, :]
                    if len(src.shape) == 3:
                        dst = dst.rearrange("p (a c) -> p a c", a=src.shape[1])
                    sp.dma_start(dst, src).then_inc(raw_in[i % 2], 16)

                def load_ctx(t):
                    sp.dma_start(rows[:, t, :], c_rows[hf, t]).then_inc(ctx_in[t], 16)

                def store_kv(k):
                    sp.wait_ge(kv_lo, hf * KVU + (k + 1))
                    s = k % 4
                    for part in range(2):
                        src = kv_out[s][:, part, :].bitcast(F32)
                        n, t = (0, k) if k < K0 else (1, k - V1)
                        sp.dma_start(
                            v_dram[4 * n:4 * n + 4, :, t, part, :].rearrange("g p d -> p g d"),
                            src.rearrange("p (g d) -> p g d", d=D)).then_inc(kv_stored[s], 16)

                sp.wait_ge(half_open, hf + 1)
                sp.dma_start(idx[:, :], pos_cols[hf], allow_slow_non_contiguous=True).then_inc(pos_in, 16)
                for t in range(TT):
                    sp.wait_ge(out_stored[t], (hf + 1) * 16)
                    load_ctx(t)
                    if t < 2:
                        load_raw(t, wv_blocks[0, t])
                load_raw(2, wv_blocks[0, 2])
                load_raw(3, wv_blocks[0, 3])
                load_raw(4, wk_heads[0])
                load_raw(5, wk_heads[1])
                load_raw(6, wv_blocks[1, 0])
                load_raw(7, wv_blocks[1, 1])

                def load_x(t):
                    sp.wait_ge(tr_done, hf * TRS + 2 * t + 2)
                    sp.dma_start(rows[:, t, :], x_rows[hf, t]).then_inc(x_in[t], 16)

                load_x(0)
                load_x(1)
                for k in range(K0):
                    store_kv(k)
                    if k + 2 < TT:
                        load_x(k + 2)
                sp.wait_ge(tr_second, hf * TRS + TR_X)
                sp.dma_start(score_i, mask_rows[hf]).then_inc(mask_in, 16)
                load_raw(8, wv_blocks[1, 2])
                load_raw(9, wv_blocks[1, 3])
                load_raw(10, wk_heads[2])
                load_raw(11, wk_heads[3])
                for h in range(KVH):
                    for c in range(CH):
                        k = K0 + 2 * h + c
                        sp.wait_ge(kv_lo, hf * KVU + (k + 1))
                        for part in range(2):
                            sp.dma_start(k_dram[h, :, part, c * CT:(c + 1) * CT],
                                         kv_out[k % 4][:, part, :].bitcast(F32)).then_inc(kv_stored[k % 4], 16)
                    if 12 + h < RAW_B0:
                        load_raw(12 + h, wk_heads[h + 4] if h + 4 < KVH else wq_heads[h + 4 - KVH])
                for k in range(V1, KVU):
                    store_kv(k)

                def load_kv(c, head, units):
                    if units is not None:
                        sp.wait_ge(ot_done, units)
                    sp.dma_start(k_parts[c].bitcast(F32),
                                 k_dram[head, :, :, c * CT:(c + 1) * CT]).then_inc(k_in[c], 16)
                    sp.dma_start(v_parts[c].bitcast(F32),
                                 v_dram[head, :, c * TT // 2:(c + 1) * TT // 2]).then_inc(v_in[c], 16)

                for s in range(4):
                    sp.wait_ge(kv_stored[s], (hf + 1) * (KVU // 4 * 32))
                load_kv(0, 0, None)
                load_kv(1, 0, None)

                def pair(p, last=False):
                    for u in range(PU):
                        if last and u % 2:
                            continue
                        src = [wo_blocks[p, 0], None, wo_blocks[p, 1], None][u]
                        if u % 2:
                            src = wq_heads[2 * (p + 1) + u // 2]
                        i = RAW_B0 + (u // 2 if last else u)
                        slot = i % 2
                        sp.wait_ge(raw_split, hf * RAWS + p * PU + i)
                        dst = raw[slot][:, :].rearrange("p (a c) -> p a c", a=src.shape[1])
                        sp.dma_start(dst, src).then_inc(raw_in[slot], 16)
                        if not last and u == 3:
                            load_kv(0, (p + 1) // 2, hf * UNITS + p * PU + 2)
                            load_kv(1, (p + 1) // 2, hf * UNITS + p * PU + 4)

                with fori(sp, 0, PAIRS - 1) as p:
                    pair(p)
                pair(PAIRS - 1, last=True)
                load_raw(RAW_C0, qweight)
                load_raw(RAW_C0 + 1, scales.rearrange("g (a n) -> g a n", a=1).broadcast_to([KT, P // KT, E]))
                sp.wait_ge(q_rot, (hf + 1) * UNITS)
                sp.dma_start(bias_rows, bias.rearrange("(a n) -> a n", a=1).broadcast_to([P, E])).then_inc(bias_in, 16)
                for t in range(TT):
                    sp.wait_ge(ffn_added, hf * TT * NH + TT + t + 1)
                    sp.dma_start(o_rows[hf, t], rows[:, t, :]).then_inc(out_stored[t], 16)
            for t in range(TT):
                sp.wait_ge(out_stored[t], (1 + HALVES) * 16)

        @block.tensor
        def _(pe):
            pe.wait_ge(ident_in, 16)
            with fori(pe, 0, HALVES) as hf:
                def weights_ready(blocks):
                    pe.wait_ge(raw_split, hf * RAWS + 1 + blocks)

                def transposes(r, tiles):
                    if r >= 2:
                        pe.wait_ge(tr_second, hf * TRS + (r - 1))
                    for i, tile in enumerate(tiles):
                        last = pe.transpose(ps[:, BK_T + r % 2, i * P:(i + 1) * P], tile, identity[:, :])
                    last.then_inc(tr_done, 1)

                def ctx_tile(t):
                    pe.wait_ge(ctx_in[t], hf * 16 + 16)
                    for g in range(2):
                        transposes(2 * t + g, [rows[:, t, (4 * g + i) * P:(4 * g + i + 1) * P] for i in range(4)])

                def norm_tile(r0, t, count):
                    pe.wait_ge(ln_rows, hf * 2 * TT + count)
                    for g in range(2):
                        transposes(r0 + 2 * t + g, [normed[t % 2][:, (4 * g + i) * P:(4 * g + i + 1) * P]
                                                    for i in range(4)])

                def kv_bank(k):
                    if k >= 2:
                        pe.wait_ge(kv_lo, hf * KVU + (k - 1))
                    return ps[:, BK_W + k % 2, :]

                def value_unit(k, t):
                    products(pe, kv_bank(k),
                             lambda i: [act_v[:, part, i, t * P:(t + 1) * P] for part in range(2)],
                             lambda i: [wv_parts[:, i, part, :] for part in range(2)], KT).then_inc(kv_done, 1)

                pe.wait_ge(half_open, hf + 1)
                ctx_tile(0)
                ctx_tile(1)
                weights_ready(RAW_V)
                for t in range(TT):
                    pe.wait_ge(tr_second, hf * TRS + 2 * t + 2)
                    value_unit(t, t)
                    if t + 2 < TT:
                        ctx_tile(t + 2)
                pe.wait_ge(table_in, hf * (16 * TT) + 16 * TT)
                for g in range(TT // 2):
                    transposes(TR_CS + g, [gathered[:, 2 * g + i // 2, (i % 2) * P:(i % 2 + 1) * P] for i in range(4)])
                with fori(pe, 0, KVH // 2) as hh:
                    for j in range(2):
                        for c in range(CH):
                            k = K0 + 2 * j + c
                            if c == 0:
                                weights_ready(hh * 2 + (RAW_B0 - RAW_A) + 7 + j)
                            pe.wait_ge(kv_lo, hf * KVU + hh * 4 + (k - 1))
                            products(pe, ps[:, BK_W + k % 2, :],
                                     lambda i: [wq_parts[:, j, i, part, :] for part in range(2)],
                                     lambda i: [act_v[:, part, i, c * CT:(c + 1) * CT] for part in range(2)],
                                     KT).then_inc(kv_done, 1)
                for t in range(TT):
                    value_unit(V1 + t, t)
                    if t >= 1:
                        norm_tile(TR_X, t - 1, t)
                norm_tile(TR_X, TT - 1, TT)

                def query_unit(v_unit, j, c, weights):
                    weights_ready(weights)
                    if v_unit is not None:
                        pe.wait_ge(q_rot, v_unit)
                    products(pe, ps[:, BK_Q, :],
                             lambda i: [wq_parts[:, j, i, part, :] for part in range(2)],
                             lambda i: [act_v[:, part, i, c * CT:(c + 1) * CT] for part in range(2)],
                             KT).then_inc(q_done, 1)

                def output_tile(part, i, c, n, fresh=False):
                    if fresh and i < 2:
                        pe.wait_ge(kv_lo, (hf + 1) * KVU)
                    else:
                        pe.wait_ge(wo_added, part + (i - 1))
                    products(pe, ps[:, BK_W + i % 2, :],
                             lambda j: [o_parts[:, c, j, l, i * P:(i + 1) * P] for l in range(2)],
                             lambda j: [wo_parts[:, n, j, l, :] for l in range(2)], 2).then_inc(wo_done, 1)

                def unit(p, u, first=False, last=False):
                    j, c = u % 2, u // 2
                    at = hf * UNITS + p * PU + u
                    pe.wait_ge(q_lo, at + 1)
                    if j == 0:
                        pe.wait_ge(k_in[c], hf * (16 * PAIRS) + p * 16 + 16)
                    for b in range(CB):
                        if not (first and u == 0):
                            pe.wait_ge(s_masked, at * 2 - 1 + b)
                        for qt in range(2):
                            q0 = b * S + qt * P
                            last_mm = products(pe, ps[:, BK_S + b, qt * S:(qt + 1) * S],
                                               lambda i: [q_parts[:, l, q0:q0 + P] for l in range(2)],
                                               lambda i: [k_parts[c][:, l, b * S:(b + 1) * S] for l in range(2)], 1)
                        last_mm.then_inc(s_done, 1)
                    if not (last and u == PU - 1):
                        nu = (u + 1) % PU
                        nj = nu % 2
                        if u == PU - 1:
                            w = p * PU + (RAW_B0 + 2)
                        elif nj == 0:
                            w = p * PU + (RAW_B0 - 2)
                        else:
                            w = p * PU + RAW_B0
                        query_unit(at + 1, nj, nu // 2, w)
                    part = hf * (PAIRS * WOS) + p * WOS + (u - 2) * 4
                    tiles = 0 if first and u < 2 else TT // CH
                    if u >= 2:
                        pe.wait_ge(ot_lo, at - u + 2)
                        w = 1 if u == 2 else 2 if last else 3
                        weights_ready(p * PU + (RAW_B0 + w))
                    elif not first:
                        pe.wait_ge(ot_lo, at - u)
                        weights_ready(p * PU + (RAW_B0 - 1))
                    for i in range(max(tiles, CB)):
                        if i < tiles:
                            output_tile(part, i, 0 if u >= 2 else 1, u % 2, fresh=first and u == 2)
                        if i < CB:
                            b = i
                            pe.wait_ge(p_ready, at * 2 + b + 1)
                            if not (first and u == 0):
                                pe.wait_ge(pt_lo, at * 2 + b - 1)
                            for kt in range(2):
                                for qt in range(2):
                                    last_t = pe.transpose(
                                        ps[:, BK_T + b, kt * S + qt * P:kt * S + (qt + 1) * P],
                                        probs_v[:, b, qt, kt * P:(kt + 1) * P], identity[:, :])
                            last_t.then_inc(pt_done, 1)
                    if j == 0:
                        pe.wait_ge(v_in[c], hf * (16 * PAIRS) + p * 16 + 16)
                    if not (first and u == 0):
                        pe.wait_ge(ot_lo, at)
                    for b in range(CB):
                        pe.wait_ge(pt_lo, at * 2 + b + 1)
                        last_mm = products(pe, ps[:, BK_O, b * S:(b + 1) * S],
                                           lambda kt: [v_parts[c][:, 2 * b + kt, l, :] for l in range(2)],
                                           lambda kt: [probs_t[:, b, kt, l, :] for l in range(2)], 2)
                    last_mm.then_inc(ot_done, 1)

                pe.wait_ge(tr_second, hf * TRS + TR_X2)
                query_unit(None, 0, 0, RAW_A + 1)
                for u in range(PU):
                    unit(0, u, first=True)
                with fori(pe, 1, PAIRS - 1) as p:
                    for u in range(PU):
                        unit(p, u)
                for u in range(PU):
                    unit(PAIRS - 1, u, last=True)
                pe.wait_ge(ot_lo, (hf + 1) * UNITS)
                weights_ready(RAW_C0)
                for n in range(NH):
                    for i in range(TT // CH):
                        output_tile(hf * (PAIRS * WOS) + (PAIRS - 1) * WOS + 8 + 4 * n, i, 1, n)

                def dense_unit(k, n, t):
                    if t == 0:
                        pe.wait_ge(w_lo, hf * (NH * KT) + (n + 1) * KT)
                    if k >= 2:
                        pe.wait_ge(ffn_added, hf * (TT * NH) + (k - 1))
                    products(pe, ps[:, BK_W + k % 2, :],
                             lambda i: [act_v[:, part, i, t * P:(t + 1) * P] for part in range(2)],
                             lambda i: [w_parts[n][:, i, part, :] for part in range(2)], KT).then_inc(ffn_done, 1)

                pe.wait_ge(pt_lo, (hf + 1) * (UNITS * CB))
                norm_tile(TR_X2, 0, TT + 1)
                norm_tile(TR_X2, 1, TT + 2)
                pe.wait_ge(wo_added, (hf + 1) * (PAIRS * WOS))
                for t in range(TT):
                    pe.wait_ge(tr_second, hf * TRS + TR_X2 + 2 * t + 2)
                    dense_unit(t, 0, t)
                    if t + 2 < TT:
                        norm_tile(TR_X2, t + 2, TT + t + 3)
                for t in range(TT):
                    dense_unit(TT + t, 1, t)

        @block.scalar
        def _(act):
            with fori(act, 0, HALVES) as hf:
                def evacuate(r, cols, first=True):
                    act.wait_ge(tr_done, hf * TRS + r + 1)
                    act.activation(cols, ps[:, BK_T + r % 2, :].rearrange("p (k t) -> p k t", t=P),
                                   ACT.Copy).then_inc(tr_first, 1)

                def tile_hi(r0, t):
                    for g in range(2):
                        evacuate(r0 + 2 * t + g, act_v[:, 0, 4 * g:4 * g + 4, t * P:(t + 1) * P])

                def split_hi(i, dst, before=None, more=0, src_shape=None):
                    if before is not None:
                        act.wait_ge(*before)
                    half_slot = hf * (RAWS // 2 * 16)
                    act.wait_ge(raw_in[i % 2], half_slot + more + (i // 2 + 1) * 16)
                    a = dst.shape[1]
                    act.activation(dst, raw[i % 2][:, :].rearrange("p (a c) -> p a c", a=a),
                                   ACT.Copy).then_inc(raw_hi, 1)

                def split_value(i, n, a, before=None):
                    split_hi(i, wv_parts[:, 2 * a:2 * a + 2, 0, :], before)

                def kv_unit_hi(k, more=0, rotated=False):
                    if k >= 4 or rotated:
                        act.wait_ge(kv_stored[k % 4], hf * (KVU // 4 * 32) + more * 32 + (k // 4) * 32)
                    if rotated:
                        act.wait_ge(k_sum, hf * (2 * KVH) + more * 4 + (k - K0 + 1))
                        act.activation(kv_out[k % 4][:, 0, :], rope_tmp[:, 0, :], ACT.Copy).then_inc(kv_hi, 1)
                    else:
                        act.wait_ge(kv_done, hf * KVU + (k + 1))
                        act.activation(kv_out[k % 4][:, 0, :], ps[:, BK_W + k % 2, :], ACT.Copy).then_inc(kv_hi, 1)

                act.wait_ge(half_open, hf + 1)
                for a in range(RAW_V):
                    split_value(a, 0, a)
                    if a % 2:
                        tile_hi(0, a // 2)
                for i in range(2):
                    split_hi(4 + i, wq_parts[:, i, :, 0, :])
                for t in range(TT):
                    kv_unit_hi(t)
                    if t + 2 < TT:
                        tile_hi(0, t + 2)
                for g in range(TT // 2):
                    r = TR_CS + g
                    act.wait_ge(tr_done, hf * TRS + r + 1)
                    act.activation(
                        rope_cos[:, 2 * g * P:(2 * g + 2) * P].rearrange("p (t q) -> p t q", t=2),
                        ps[:, BK_T + r % 2, :].rearrange("p (t w q) -> p t w q", t=2, w=2)[:, :, 0, :],
                        ACT.Copy).then_inc(tr_first, 1)
                for a in range(RAW_V):
                    split_value(6 + a, 1, a, (kv_done, hf * KVU + K0))
                act.wait_ge(ln_var, hf * 2 + 1)
                act.activation(ln_tmp[:, 1, :], ln_tmp[:, 0, :], ACT.Sqrt).then_inc(ln_root, 1)
                with fori(act, 0, KVH // 2) as hh:
                    for j in range(2):
                        for c in range(CH):
                            kv_unit_hi(K0 + 2 * j + c, more=hh, rotated=True)
                        split_hi(10 + j, wq_parts[:, j, :, 0, :],
                                 (kv_done, hf * KVU + hh * 4 + K0 + 2 * j + 2), more=hh * 16)
                for t in range(TT):
                    kv_unit_hi(V1 + t)
                    if t >= 1:
                        tile_hi(TR_X, t - 1)
                tile_hi(TR_X, TT - 1)

                def query_hi(count):
                    act.wait_ge(q_sum, count)
                    act.activation(q_parts[:, 0, :], rope_tmp[:, 0, :], ACT.Copy).then_inc(q_hi, 1)

                def unit(p, u, first=False, last=False):
                    j, c = u % 2, u // 2
                    at = hf * UNITS + p * PU + u
                    for b in range(CB):
                        act.wait_ge(max_ready, at * 2 + b + 1)
                        if not (first and u == 0):
                            act.wait_ge(pt_done, at * 2 + b - 1)
                        for qt in range(2):
                            i = 2 * b + qt
                            e = act.activation(probs_v[:, b, qt, :], score_v[:, 2 * c + b, qt, :], ACT.Exp,
                                               bias=neg_max[:, i:i + 1], scale=SCALE,
                                               accum_out=row_sum[:, i:i + 1])
                        e.then_inc(exp_done, 1)
                    for b in range(CB):
                        act.wait_ge(inv_ready, at * 2 + b + 1)
                        for qt in range(2):
                            i = 2 * b + qt
                            e = act.activation(probs_v[:, b, qt, :], probs_v[:, b, qt, :], ACT.Copy,
                                               scale=inv_sum[:, i:i + 1])
                        e.then_inc(p_ready, 1)

                    def split(v, dst, before):
                        i = RAW_B0 + v
                        split_hi(i, dst, before, more=p * 32)

                    if u == 2:
                        split(2 if not last else 1, wo_parts[:, 1, :, 0, :],
                              None if first else (wo_done, hf * (PAIRS * WOS) + p * WOS))
                    if u == 3 and not last:
                        split(3, wq_parts[:, 1, :, 0, :], (q_done, at + 1))
                    for b in range(CB):
                        act.wait_ge(pt_done, at * 2 + b + 1)
                        act.activation(probs_t[:, b, :, 0, :], ps[:, BK_T + b, :].rearrange("p (k q) -> p k q", k=2),
                                       ACT.Copy).then_inc(pt_hi, 1)
                    if not (last and u == PU - 1):
                        query_hi(at + 2)
                    if u == 0:
                        split(0, wo_parts[:, 0, :, 0, :],
                              None if first else (wo_done, hf * (PAIRS * WOS) + p * WOS - 4))
                    if u == 1 and not last:
                        split(1, wq_parts[:, 0, :, 0, :], (q_done, at + 2))
                    act.wait_ge(ot_done, at + 1)
                    act.activation(o_parts[:, c, j, 0, :], ps[:, BK_O, :], ACT.Copy).then_inc(ot_hi, 1)

                query_hi(hf * UNITS + 1)
                for u in range(PU):
                    unit(0, u, first=True)
                with fori(act, 1, PAIRS - 1) as p:
                    for u in range(PU):
                        unit(p, u)
                for u in range(PU):
                    unit(PAIRS - 1, u, last=True)

                act.wait_ge(ln_var, hf * 2 + 2)
                act.activation(ln_tmp[:, 1, :], ln_tmp[:, 0, :], ACT.Sqrt).then_inc(ln_root, 1)

                def weight_hi(n, i):
                    act.wait_ge(w_full, hf * (NH * KT) + n * KT + i + 1)
                    act.activation(w_parts[n][:, i, 0, :], w_f32, ACT.Copy).then_inc(w_hi, 1)

                for i in range(KT):
                    weight_hi(0, i)
                tile_hi(TR_X2, 0)
                tile_hi(TR_X2, 1)
                act.wait_ge(wo_done, (hf + 1) * (PAIRS * WOS))
                for t in range(TT):
                    if t + 2 < TT:
                        tile_hi(TR_X2, t + 2)
                    weight_hi(1, t)

        @block.vector
        def _(dve):
            with fori(dve, 0, HALVES) as hf:
                def lo(dst, src, hi, sem_, value, done):
                    dve.wait_ge(sem_, value)
                    dve.tensor_tensor(dst, src, hi.bitcast(F32), ALU.subtract).then_inc(done, 1)

                def tile_lo(r0, t):
                    for g in range(2):
                        r = r0 + 2 * t + g
                        lo(act_v[:, 1, 4 * g:4 * g + 4, t * P:(t + 1) * P],
                           ps[:, BK_T + r % 2, :].rearrange("p (k t) -> p k t", t=P),
                           act_v[:, 0, 4 * g:4 * g + 4, t * P:(t + 1) * P],
                           tr_first, hf * TRS + r + 1, tr_second)

                def rotate(bank, t0, done):
                    dve.tensor_tensor(rope_tmp[:, 0, :], ps[:, bank, :], rope_cos[:, t0:t0 + CT], ALU.mult)
                    dve.tensor_tensor(rope_tmp[0:HD2, 1, :], ps[HD2:D, bank, :], rope_sin[HD2:D, t0:t0 + CT],
                                      ALU.mult)
                    dve.tensor_tensor(rope_tmp[HD2:D, 1, :], ps[0:HD2, bank, :], rope_sin[0:HD2, t0:t0 + CT],
                                      ALU.mult).then_inc(done, 1)

                def value_lo(k):
                    lo(kv_out[k % 4][:, 1, :], ps[:, BK_W + k % 2, :], kv_out[k % 4][:, 0, :],
                       kv_hi, hf * KVU + k + 1, kv_lo)

                def tile_stats(t):
                    for n in range(NH):
                        dve.bn_stats(stats[:, t, n, :], rows[:, t, n * NW:(n + 1) * NW]).then_inc(ln_chain, 1)

                def inverse_std(which):
                    before = hf * LN_LINKS + which * (LN_LINKS // 2)
                    dve.wait_ge(ln_chain, before + 2 * TT)
                    hold(dve)
                    for t in range(TT):
                        dve.bn_aggr(mean_var[:, t, :], stats[:, t, :, :]).then_inc(ln_chain, 1)
                    dve.wait_ge(ln_chain, before + 3 * TT)
                    dve.tensor_scalar(ln_tmp[:, 0, :], mean_var[:, :, 1], EPS, None, ALU.add).then_inc(ln_var, 1)
                    dve.wait_ge(ln_root, hf * 2 + which + 1)
                    y, w, v = ln_tmp[:, 2, :], ln_tmp[:, 3, :], ln_tmp[:, 0, :]
                    steps = [
                        lambda: dve.reciprocal(y, ln_tmp[:, 1, :]),
                        lambda: dve.tensor_tensor(w, y, y, ALU.mult),
                        lambda: dve.tensor_tensor(w, w, v, ALU.mult),
                        lambda: dve.tensor_scalar(w, w, -0.5, 1.5, ALU.mult, ALU.add),
                        lambda: dve.tensor_tensor(inv_std[:, :], y, w, ALU.mult),
                    ]
                    for i, step in enumerate(steps):
                        step().then_inc(ln_chain, 1)
                        dve.wait_ge(ln_chain, before + 3 * TT + i + 1)
                    hold(dve)

                def normalize(t, which):
                    if t >= 2:
                        dve.wait_ge(tr_done, hf * TRS + (TR_X, TR_X2)[which] + 2 * (t - 1))
                    dst = normed[t % 2]
                    src = rows[:, t, :]
                    if which:
                        dst = dst.rearrange("p (j r) -> p j r", j=NIB)
                        src = src.rearrange("p (r j) -> p j r", j=NIB)
                    dve.tensor_scalar(dst, src, mean_var[:, t, 0:1], inv_std[:, t:t + 1],
                                      ALU.subtract, ALU.mult).then_inc(ln_rows, 1)

                dve.wait_ge(pos_in, hf * 16 + 16)
                dve.tensor_scalar(idx_neg[:, :], idx[:, :], 0, MAX_POS, ALU.is_lt, ALU.mult).then_inc(idx_step, 1)
                dve.wait_ge(idx_step, hf * 2 + 1)
                hold(dve)
                dve.tensor_tensor(idx[:, :], idx[:, :], idx_neg[:, :], ALU.add).then_inc(idx_step, 1)
                dve.wait_ge(idx_step, hf * 2 + 2)
                dve.tensor_scalar(idx[:, :], idx[:, :], 0, MAX_POS - 1, ALU.max, ALU.min).then_inc(idx_ready, 1)
                for t in range(2):
                    tile_lo(0, t)
                for t in range(TT):
                    value_lo(t)
                    if t + 2 < TT:
                        tile_lo(0, t + 2)
                for g in range(TT // 2):
                    r = TR_CS + g
                    dve.wait_ge(tr_first, hf * TRS + r + 1)
                    dve.tensor_copy(
                        rope_sin[:, 2 * g * P:(2 * g + 2) * P].rearrange("p (t q) -> p t q", t=2),
                        ps[:, BK_T + r % 2, :].rearrange("p (t w q) -> p t w q", t=2, w=2)[:, :, 1, :],
                    ).then_inc(tr_second, 1)
                for t in range(TT):
                    dve.wait_ge(x_in[t], hf * 16 + 16)
                    tile_stats(t)
                inverse_std(0)
                with fori(dve, 0, KVH // 2) as hh:
                    for j in range(2):
                        for c in range(CH):
                            k = K0 + 2 * j + c
                            n = 2 * j + c
                            dve.wait_ge(kv_done, hf * KVU + hh * 4 + k + 1)
                            dve.wait_ge(tr_second, hf * TRS + TR_X)
                            dve.wait_ge(kv_lo, hf * KVU + hh * 4 + k)
                            rotate(BK_W + k % 2, c * CT, k_rot)
                            lo(kv_out[k % 4][:, 1, :], rope_tmp[:, 0, :], kv_out[k % 4][:, 0, :],
                               kv_hi, hf * KVU + hh * 4 + k + 1, kv_lo)
                dve.wait_ge(mask_in, hf * 16 + 16)
                dve.tensor_scalar(mask_v, score_i, 0, None, ALU.not_equal).then_inc(mask_ready, 1)
                dve.wait_ge(mask_ready, hf + 1)
                dve.memset(scores[:, :], MASKED).then_inc(fill_done, 1)
                dve.wait_ge(fill_done, hf + 1)
                dve.wait_ge(kv_lo, hf * KVU + V1)
                for t in range(2):
                    normalize(t, 0)
                for t in range(TT):
                    value_lo(V1 + t)
                    if t >= 1:
                        tile_lo(TR_X, t - 1)
                        if t + 1 < TT:
                            normalize(t + 1, 0)
                tile_lo(TR_X, TT - 1)

                def query_products(count, c, first=False):
                    dve.wait_ge(q_done, count)
                    if not first:
                        dve.wait_ge(q_lo, count - 1)
                    rotate(BK_Q, c * CT, q_rot)

                def query_lo(count):
                    lo(q_parts[:, 1, :], rope_tmp[:, 0, :], q_parts[:, 0, :], q_hi, count, q_lo)

                def add_output(k, t, n):
                    dve.wait_ge(wo_done, k + 1)
                    dst = rows[:, t, n * NW:(n + 1) * NW]
                    dve.tensor_tensor(dst, ps[:, BK_W + t % 2, :], dst, ALU.add).then_inc(wo_added, 1)

                def unit(p, u, first=False, last=False):
                    j, c = u % 2, u // 2
                    at = hf * UNITS + p * PU + u
                    for b in range(CB):
                        dve.wait_ge(s_done, at * 2 + b + 1)
                        if not (first and u == 0):
                            dve.wait_ge(exp_done, at * 2 + b - 1)
                        hold(dve)
                        dve.copy_predicated(score_v[:, 2 * c + b, :, :], mask_v[:, 2 * c + b, :, :],
                                            ps[:, BK_S + b, :].rearrange("p (q k) -> p q k", q=2)
                                            ).then_inc(s_masked, 1)
                    for b in range(CB):
                        dve.wait_ge(s_masked, at * 2 + b + 1)
                        dve.tensor_reduce(row_max[:, 2 * b:2 * b + 2], score_v[:, 2 * c + b, :, :], AX.X,
                                          ALU.max).then_inc(max_done, 1)
                    for b in range(CB):
                        dve.wait_ge(max_done, at * 2 + b + 1)
                        dve.tensor_scalar(neg_max[:, 2 * b:2 * b + 2], row_max[:, 2 * b:2 * b + 2], -SCALE, None,
                                          ALU.mult).then_inc(max_ready, 1)
                    for b in range(CB):
                        dve.wait_ge(exp_done, at * 2 + b + 1)
                        dve.reciprocal(inv_sum[:, 2 * b:2 * b + 2], row_sum[:, 2 * b:2 * b + 2]).then_inc(inv_ready, 1)
                    more = not (last and u == PU - 1)
                    if more:
                        query_products(at + 2, ((u + 1) % PU) // 2)
                    k0 = hf * (PAIRS * WOS) + p * WOS + (u - 2) * 4
                    t0, n = (0, u - 2) if u >= 2 else (TT // 2, u)
                    adds = 0 if first and u < 2 else 4
                    for i in range(4):
                        if i < adds:
                            add_output(k0 + i, t0 + i, n)
                        if i < CB:
                            lo(probs_t[:, i, :, 1, :], ps[:, BK_T + i, :].rearrange("p (k q) -> p k q", k=2),
                               probs_t[:, i, :, 0, :], pt_hi, at * 2 + i + 1, pt_lo)
                        if i == CB and more:
                            query_lo(at + 2)
                    lo(o_parts[:, c, j, 1, :], ps[:, BK_O, :], o_parts[:, c, j, 0, :], ot_hi, at + 1, ot_lo)

                dve.wait_ge(tr_second, hf * TRS + TR_X2)
                query_products(hf * UNITS + 1, 0, first=True)
                query_lo(hf * UNITS + 1)
                for u in range(PU):
                    unit(0, u, first=True)
                with fori(dve, 1, PAIRS - 1) as p:
                    for u in range(PU):
                        unit(p, u)
                for u in range(PU):
                    unit(PAIRS - 1, u, last=True)
                for n in range(NH):
                    for i in range(4):
                        add_output(hf * (PAIRS * WOS) + (PAIRS - 1) * WOS + 8 + 4 * n + i, TT // 2 + i, n)

                dve.wait_ge(wo_added, (hf + 1) * (PAIRS * WOS))
                for t in range(TT):
                    tile_stats(t)
                inverse_std(1)
                dve.wait_ge(exp_done, (hf + 1) * (UNITS * CB))
                dve.wait_ge(p_ready, (hf + 1) * (UNITS * CB))
                dve.wait_ge(pt_done, (hf + 1) * (UNITS * CB))
                dve.wait_ge(q_lo, (hf + 1) * UNITS)
                for t in range(2):
                    normalize(t, 1)
                dve.wait_ge(zero_words_in, 16)
                for i in range(NIB):
                    dve.tensor_scalar(zeros_i.rearrange("p (w i) -> p w i", i=NIB)[:, :, i], zero_words[:, :],
                                      BITS * i, 2 ** BITS - 1, ALU.logical_shift_right,
                                      ALU.bitwise_and).then_inc(z_step, 1)
                dve.wait_ge(z_step, (hf + 1) * NIB)
                raw_c = hf * (RAWS // 2 * 16) + (RAW_C0 // 2 + 1) * 16
                dve.wait_ge(raw_in[0], raw_c)
                dve.wait_ge(raw_in[1], raw_c)

                def weights(n, i):
                    cols = slice(n * NW, (n + 1) * NW)
                    k = hf * (NH * KT) + n * KT + i
                    if n or i:
                        dve.wait_ge(w_lo, k)
                    dve.tensor_scalar(w_int, raw_i[0][:, cols], BITS * i, 2 ** BITS - 1,
                                      ALU.logical_shift_right, ALU.bitwise_and).then_inc(w_step, 1)
                    dve.wait_ge(w_step, k * 2 + 1)
                    dve.tensor_tensor(w_f32, w_int, zeros_i[:, cols], ALU.subtract).then_inc(w_step, 1)
                    dve.wait_ge(w_step, k * 2 + 2)
                    dve.tensor_tensor(w_f32, w_f32, raw[1][:, cols], ALU.mult).then_inc(w_full, 1)
                    lo(w_parts[n][:, i, 1, :], w_f32, w_parts[n][:, i, 0, :], w_hi, k + 1, w_lo)

                for i in range(KT):
                    weights(0, i)
                def add_dense(k, t, n):
                    dve.wait_ge(ffn_done, hf * (TT * NH) + k + 1)
                    if n == 0:
                        dve.wait_ge(biased, hf * TT + t + 1)
                    dst = rows[:, t, n * NW:(n + 1) * NW]
                    dve.tensor_tensor(dst, ps[:, BK_W + k % 2, :], dst, ALU.add).then_inc(ffn_added, 1)

                for t in range(2):
                    tile_lo(TR_X2, t)
                for t in range(TT):
                    if t + 2 < TT:
                        normalize(t + 2, 1)
                        tile_lo(TR_X2, t + 2)
                    add_dense(t, t, 0)
                    weights(1, t)
                for t in range(TT):
                    add_dense(TT + t, t, 1)
                dve.wait_ge(ffn_added, (hf + 1) * (TT * NH))
                dve.sem_inc(half_open, 1)

        @block.gpsimd
        def _(pool):
            with fori(pool, 0, HALVES) as hf:
                def split_lo(i, dst, hi, more=0):
                    pool.wait_ge(raw_hi, hf * (RAWS - 2) + more + i + 1)
                    a = dst.shape[1]
                    pool.tensor_tensor(dst, raw[i % 2][:, :].rearrange("p (a c) -> p a c", a=a),
                                       hi.bitcast(F32), ALU.subtract).then_inc(raw_split, 1)

                def split_value(i, a):
                    split_lo(i, wv_parts[:, 2 * a:2 * a + 2, 1, :], wv_parts[:, 2 * a:2 * a + 2, 0, :])

                def rope_sum(wait, value, done):
                    pool.wait_ge(wait, value)
                    pool.tensor_tensor(rope_tmp[:, 0, :], rope_tmp[:, 0, :], rope_tmp[:, 1, :],
                                       ALU.add).then_inc(done, 1)

                for a in range(RAW_V):
                    split_value(a, a)
                pool.wait_ge(idx_ready, hf + 1)
                pool.wait_ge(half_open, hf + 1)
                hold(pool)
                for t in range(TT):
                    pool.indirect_dma_start(gathered[:, t, :], None, table,
                                            bass.IndirectOffsetOnAxis(ap=idx[:, t:t + 1], axis=0)
                                            ).then_inc(table_in, 16)
                for i in range(2):
                    split_lo(4 + i, wq_parts[:, i, :, 1, :], wq_parts[:, i, :, 0, :])
                for a in range(RAW_V):
                    split_value(6 + a, a)
                with fori(pool, 0, KVH // 2) as hh:
                    for j in range(2):
                        for c in range(CH):
                            n = 2 * j + c
                            rope_sum(k_rot, hf * (2 * KVH) + hh * 4 + n + 1, k_sum)
                        split_lo(10 + j, wq_parts[:, j, :, 1, :], wq_parts[:, j, :, 0, :], more=hh * 2)

                def unit(p, u, first=False, last=False):
                    at = hf * UNITS + p * PU + u

                    def split(v, dst, hi):
                        split_lo(RAW_B0 + v, dst, hi, more=p * PU)

                    if u == 2:
                        split(2 if not last else 1, wo_parts[:, 1, :, 1, :], wo_parts[:, 1, :, 0, :])
                    if u == 3 and not last:
                        split(3, wq_parts[:, 1, :, 1, :], wq_parts[:, 1, :, 0, :])
                    if not (last and u == PU - 1):
                        rope_sum(q_rot, at + 2, q_sum)
                    if u == 0:
                        split(0, wo_parts[:, 0, :, 1, :], wo_parts[:, 0, :, 0, :])
                    if u == 1 and not last:
                        split(1, wq_parts[:, 0, :, 1, :], wq_parts[:, 0, :, 0, :])

                rope_sum(q_rot, hf * UNITS + 1, q_sum)
                for u in range(PU):
                    unit(0, u, first=True)
                with fori(pool, 1, PAIRS - 1) as p:
                    for u in range(PU):
                        unit(p, u)
                for u in range(PU):
                    unit(PAIRS - 1, u, last=True)

                pool.wait_ge(bias_in, hf * 16 + 16)
                for t in range(TT):
                    pool.wait_ge(ln_rows, hf * 2 * TT + TT + t + 1)
                    pool.tensor_tensor(rows[:, t, :], rows[:, t, :], bias_rows, ALU.add).then_inc(biased, 1)
                pool.wait_ge(w_full, (hf + 1) * (NH * KT))
                pool.sem_inc(raw_split, 2)


LN_LINKS = 2 * (3 * TT + 5)

_INS = ["x", "ctx_4096", "pos_BxS2", "mask_BxSxS2_ik0", "L0_xattn_Wq", "L0_xattn_Wk", "L0_xattn_Wv",
        "L0_xattn_Wo", "L0_ffn_qweight", "L0_ffn_qzeros", "L0_ffn_scales", "L0_ffn_bias"]


def kernel(**inputs):
    import concourse.bacc as bacc
    from concourse.bass_utils import run_bass_kernel_spmd

    nc = bacc.Bacc("TRN2", target_bir_lowering=False, num_devices=1)
    arrays = {f"in_{name}": np.ascontiguousarray(inputs[name]) for name in _INS}
    arrays["in_rope_table"] = rope_table()
    arrays["in_identity"] = np.eye(P, dtype=np.float32)
    args = [nc.dram_tensor(name, a.shape, mybir.dt.from_np(a.dtype), kind="ExternalInput").ap()
            for name, a in arrays.items()]
    out = nc.dram_tensor("out", (B, S, E), F32, kind="ExternalOutput").ap()
    build(nc, *args, out)
    result = run_bass_kernel_spmd(nc, [arrays], core_ids=[0])
    return result.results[0]["out"]
```

```python
from contextlib import ExitStack

import numpy as np

import concourse.bass as bass
from concourse import mybir

ALU = mybir.AluOpType
ACT = mybir.ActivationFunctionType
F32 = mybir.dt.float32
F32R = mybir.dt.float32r
I32 = mybir.dt.int32
U8 = mybir.dt.uint8
AX = mybir.AxisListType

P = 128
E = 1024
KT = E // P
B, S = 8, 256
H, KVH, D = 32, 8, 128
HD2 = D // 2
HALVES = 2
HB = B // HALVES
T = HB * S
TT = T // P
CH = 2
CB = HB // CH
CT = T // CH
NW = 512
NH = E // NW
PAIRS = H // 2
PU = 4
UNITS = PAIRS * PU
MAX_POS, THETA = 1024, 10000.0
SCALE = float(np.float32(1.0) / np.sqrt(np.float32(D)))
MASKED = float(np.float32(-1e9) * np.sqrt(np.float32(D)))
EPS = 1e-5
BITS = 4
NIB = 32 // BITS
RAW_V = 4
RAW_K = RAW_V + 2
RAW_B0 = RAW_K + 4 * (KVH // 2)
RAW_C0 = RAW_B0 + PAIRS * PU - 2
RAWS = RAW_C0 + NH * RAW_V
RING = (RAWS - 2) // 2
DENSE_ORDER = (2, 0, 1, 3)
KVU = 2 * TT + 2 * KVH
K0 = TT
V1 = TT + 2 * KVH
TR_CS, TR_X = 2 * TT, 2 * TT + TT // 2
TR_X2 = TR_X + 2 * TT
TRS = TR_X2 + 2 * TT
WOS = TT * NH
WC = E // (KVH // 2)
LN_A = 3 * TT + 5
LN_C = 3 * 2 + 5
LN_LINKS = LN_A + (TT // 2) * LN_C
BK_S, BK_Q, BK_T, BK_O, BK_W = 0, 2, 3, 5, 6


def rope_table():
    steps = np.arange(0, D, 2, dtype=np.float32) / np.float32(D)
    inv_freq = np.float32(1) / np.power(THETA, steps.astype(np.float64)).astype(np.float32)
    freqs = np.arange(MAX_POS, dtype=np.float32)[:, None] * inv_freq[None]
    cos = np.cos(freqs.astype(np.float64)).astype(np.float32)
    sin = np.sin(freqs.astype(np.float64)).astype(np.float32)
    return np.concatenate([cos, cos, sin, -sin], axis=1)


def build(nc, x, ctx4, pos, mask, wq, wk, wv, wo, qweight, qzeros, scales, bias, table, ident, out):
    x_rows = x.rearrange("b s e -> (b s) e").rearrange("(h t p) e -> h t p e", p=P, t=TT)
    c_rows = ctx4.rearrange("b s e -> (b s) e").rearrange("(h t p) e -> h t p e", p=P, t=TT)
    o_rows = out.rearrange("b s e -> (b s) e").rearrange("(h t p) e -> h t p e", p=P, t=TT)
    pos_cols = pos.rearrange("b s -> (b s)").rearrange("(h t p) -> h p t", p=P, t=TT)
    mask_rows = mask.rearrange("(h b) (q p) k -> h p b q k", p=P, b=HB)
    wq_heads = wq.rearrange("(k p) (h d) -> h p k d", p=P, d=D)
    wk_heads = wk.rearrange("(k p) (h d) -> h p k d", p=P, d=D)
    wv_rows = wv.rearrange("(k p) (n c) -> n k p c", p=P, c=NW)
    wv_blocks = wv.rearrange("(a k p) (n c) -> n a p k c", p=P, k=KT // RAW_V, c=NW)
    packed_cols = qweight.rearrange("p (g c) -> g p c", c=WC)
    scale_cols = scales.rearrange("r (g c) -> g r c", c=WC)
    wo_blocks = wo.rearrange("(j t p) (n c) -> j n p t c", p=P, t=2, c=NW)

    with ExitStack() as stack:
        def sb(name, shape, dt):
            return stack.enter_context(nc.sbuf_tensor(name, shape, dt))

        def sem(name):
            return stack.enter_context(nc.semaphore(name))

        act_t = sb("act_t", [P, 2 * KT * T], F32R)
        parts = sb("parts", [P, 16384], F32R)
        rows = sb("rows", [P, TT, E], F32)
        raw = [sb(f"raw{i}", [P, E], F32) for i in range(2)]
        q_parts = sb("q_parts", [P, 2, CT], F32R)
        rope_cos = sb("rope_cos", [P, T], F32)
        rope_sin = sb("rope_sin", [P, T], F32)
        scores = sb("scores", [P, HB * 2 * S], F32)
        mask8 = sb("mask8", [P, HB * 2, S], U8)
        probs = sb("probs", [P, CB * 2 * S], F32)
        probs_t = sb("probs_t", [P, CB, 2, 2, S], F32R)
        rope_tmp = sb("rope_tmp", [P, 2, NW], F32)
        identity = sb("identity", [P, P], F32)
        idx = sb("idx", [P, TT], I32)
        idx_neg = sb("idx_neg", [P, TT], I32)
        zero_words = sb("zero_words", [P, E // NIB], I32)
        stats = sb("stats", [P, TT, NH, 6], F32)
        mean_var = sb("mean_var", [P, TT, 2], F32)
        ln_tmp = sb("ln_tmp", [P, 4, TT], F32)
        inv_std = sb("inv_std", [P, TT], F32)
        row_max = sb("row_max", [P, 4], F32)
        neg_max = sb("neg_max", [P, 4], F32)
        row_sum = sb("row_sum", [P, 4], F32)
        inv_sum = sb("inv_sum", [P, 4], F32)
        ps = stack.enter_context(nc.psum_tensor("ps", [P, 8, NW], F32))
        k_dram = nc.dram_tensor("k_scratch", [KVH, P, 2, T], F32, kind="Internal").ap()
        v_dram = nc.dram_tensor("v_scratch", [KVH, P, TT, 2, D], F32, kind="Internal").ap()

        w_dram = nc.dram_tensor("w_scratch", [KT, P, E], F32, kind="Internal").ap()

        act_v = act_t[:, :].rearrange("p (l k t) -> p l k t", l=2, k=KT)
        o_parts = parts[:, 0:4096].rearrange("p (c j l t) -> p c j l t", c=CH, j=2, l=2)
        wo_parts = parts[:, 4096:8192].rearrange("p (n j l c) -> p n j l c", n=NH, j=2, l=2)
        wq_parts = parts[:, 8192:12288].rearrange("p (s k l d) -> p s k l d", s=2, k=KT, l=2)
        kv_parts = parts[:, 12288:16384]
        k_parts = [kv_parts[:, c * 2048:c * 2048 + 1024].rearrange("p (l t) -> p l t", l=2) for c in range(CH)]
        v_parts = [kv_parts[:, c * 2048 + 1024:c * 2048 + 2048].rearrange("p (t l d) -> p t l d", l=2, d=D)
                   for c in range(CH)]
        kv_out = [kv_parts[:, s * 1024:(s + 1) * 1024].rearrange("p (l t) -> p l t", l=2) for s in range(4)]
        wv_parts = parts[:, 0:8192].rearrange("p (k l c) -> p k l c", k=KT, l=2)
        w_parts = [parts[:, 8192:16384].rearrange("p (k l c) -> p k l c", k=KT, l=2), wv_parts]
        score_v = scores[:, :].rearrange("p (b q k) -> p b q k", b=HB, q=2)
        mask_v = mask8[:, :, :].rearrange("p (b q) k -> p b q k", b=HB)
        gathered = scores[:, :].rearrange("p (t c) -> p t c", t=TT)
        probs_v = probs[:, :].rearrange("p (b q k) -> p b q k", b=CB, q=2)
        normed = [probs[:, :], rope_tmp[:, :, :].rearrange("p a n -> p (a n)")]
        value_raw = [b.rearrange("p (a c) -> p a c", a=2) for b in (raw[0][:, :], raw[1][:, :], *normed)]
        x_normed = [probs[:, :], scores[:, CB * 2 * S:]]
        mask_i = probs[:, :].bitcast(I32).rearrange("p (b q k) -> p b q k", b=CB, q=2)
        zeros_i = scores[:, 0:E].bitcast(I32)
        packed = scores[:, E:E + WC].bitcast(I32)
        scale_rows = scores[:, E + WC:E + 2 * WC]
        dense_w = [probs[:, i * 2 * WC:(i + 1) * 2 * WC].rearrange("p (j c) -> p j c", j=2) for i in range(2)]
        bias_rows = rope_cos[:, 0:E]

        ident_in, zero_words_in = sem("ident_in"), sem("zero_words_in")
        half_open = sem("half_open")
        held = sem("held")
        pos_in, mask_in, bias_in = sem("pos_in"), sem("mask_in"), sem("bias_in")
        ctx_in = [sem(f"ctx_in{t}") for t in range(TT)]
        x_in = [sem(f"x_in{t}") for t in range(TT)]
        raw_in = [sem(f"raw_in{i}") for i in range(RAW_V)]
        table_in = sem("table_in")
        kv_stored = [sem(f"kv_stored{s}") for s in range(4)]
        k_in = [sem(f"k_in{c}") for c in range(CH)]
        v_in = [sem(f"v_in{c}") for c in range(CH)]
        out_stored = [sem(f"out_stored{t}") for t in range(TT)]
        raw_hi, raw_split = sem("raw_hi"), sem("raw_split")
        tr_done, tr_first, tr_second = sem("tr_done"), sem("tr_first"), sem("tr_second")
        idx_ready, idx_step = sem("idx_ready"), sem("idx_step")
        packed_in, scale_in = sem("packed_in"), sem("scale_in")
        w_stored = [sem(f"w_stored{i}") for i in range(2)]
        mask_ready, fill_done = sem("mask_ready"), sem("fill_done")
        kv_done, kv_hi, kv_lo = sem("kv_done"), sem("kv_hi"), sem("kv_lo")
        k_rot, k_sum = sem("k_rot"), sem("k_sum")
        ln_chain, ln_var, ln_root, ln_rows = sem("ln_chain"), sem("ln_var"), sem("ln_root"), sem("ln_rows")
        q_done, q_rot, q_sum, q_hi, q_lo = sem("q_done"), sem("q_rot"), sem("q_sum"), sem("q_hi"), sem("q_lo")
        s_done, s_masked, max_done, max_ready = sem("s_done"), sem("s_masked"), sem("max_done"), sem("max_ready")
        exp_done, inv_ready, p_ready = sem("exp_done"), sem("inv_ready"), sem("p_ready")
        pt_done, pt_hi, pt_lo = sem("pt_done"), sem("pt_hi"), sem("pt_lo")
        ot_done, ot_hi, ot_lo = sem("ot_done"), sem("ot_hi"), sem("ot_lo")
        wo_done, wo_added = sem("wo_done"), sem("wo_added")
        z_step, biased = sem("z_step"), sem("biased")
        w_step, w_full = sem("w_step"), sem("w_full")
        ffn_done, ffn_added = sem("ffn_done"), sem("ffn_added")

        block = stack.enter_context(nc.Block())

        def hold(eng):
            eng.sem_inc(held, 1)

        def products(eng, dst, left, right, n):
            for k in range(n):
                lh, ll = left(k)
                rh, rl = right(k)
                eng.matmul(dst, lh, rh, start=(k == 0), stop=False)
                eng.matmul(dst, lh, rl, start=False, stop=False)
                last = eng.matmul(dst, ll, rh, start=False, stop=(k == n - 1))
            return last

        @block.sync
        def _(sp):
            sp.dma_start(identity[:, :], ident).then_inc(ident_in, 16)
            sp.dma_start(zero_words[:, :],
                         qzeros.rearrange("g (a w) -> g a w", a=1).broadcast_to([KT, P // KT, E // NIB])
                         ).then_inc(zero_words_in, 16)
            for t in range(TT):
                sp.sem_inc(out_stored[t], 16)
            sp.sem_inc(raw_split, 1)
            sp.sem_inc(half_open, 1)
            sp.sem_inc(w_full, 1)
            for i in range(2):
                sp.sem_inc(w_stored[i], 16)
            with sp.Fori(0, HALVES) as hf:
                def load_raw(i, src):
                    if i < 2 or i >= RAW_V:
                        sp.wait_ge(raw_split, hf * RAWS + 1 + max(i - 1, 0))
                    if i < RAW_V:
                        sp.dma_start(value_raw[i], src).then_inc(raw_in[i], 16)
                        return
                    dst = raw[i % 2][:, 0:src.shape[1] * src.shape[2]].rearrange("p (a c) -> p a c", a=src.shape[1])
                    sp.dma_start(dst, src).then_inc(raw_in[i % 2], 16)

                def load_ctx(t):
                    sp.dma_start(rows[:, t, :], c_rows[hf, t]).then_inc(ctx_in[t], 16)

                def store_kv(k):
                    sp.wait_ge(kv_lo, hf * KVU + (k + 1))
                    s = k % 4
                    for part in range(2):
                        src = kv_out[s][:, part, :].bitcast(F32)
                        n, t = (0, k) if k < K0 else (1, k - V1)
                        sp.dma_start(
                            v_dram[4 * n:4 * n + 4, :, t, part, :].rearrange("g p d -> p g d"),
                            src.rearrange("p (g d) -> p g d", d=D)).then_inc(kv_stored[s], 16)

                for t in range(TT):
                    sp.wait_ge(out_stored[t], (hf + 1) * 16)
                    load_ctx(t)
                    if t == 0:
                        for i in range(RAW_V):
                            load_raw(i, wv_blocks[0, i])
                        sp.dma_start(idx[:, :], pos_cols[hf], allow_slow_non_contiguous=True).then_inc(pos_in, 16)
                load_raw(4, wk_heads[0])
                load_raw(5, wk_heads[1])

                def load_x(t):
                    sp.wait_ge(tr_done, hf * TRS + 2 * t + 2)
                    sp.dma_start(rows[:, t, :], x_rows[hf, t]).then_inc(x_in[t], 16)

                def load_mask(c):
                    sp.dma_start(mask_i, mask_rows[hf][:, c * CB:(c + 1) * CB]).then_inc(mask_in, 16)

                load_x(0)
                load_x(1)
                sp.wait_ge(raw_split, hf * RAWS + 1 + RAW_V)
                load_mask(0)
                for k in range(K0):
                    store_kv(k)
                    if k == 3:
                        sp.wait_ge(mask_ready, hf * CH + 1)
                        load_mask(1)
                    if k + 2 < TT:
                        load_x(k + 2)
                sp.wait_ge(tr_second, hf * TRS + TR_X)
                def load_packed(hh):
                    sp.dma_start(packed, packed_cols[hh]).then_inc(packed_in, 16)
                    sp.dma_start(scale_rows, scale_cols[hh].rearrange("r (a n) -> r a n", a=1)
                                 .broadcast_to([KT, P // KT, WC])).then_inc(scale_in, 16)

                load_packed(0)
                hold(sp)
                def key_heads(hh, next_head, last=False):
                    def load_block(v, src):
                        sp.wait_ge(raw_split, hf * RAWS + hh * 4 + (RAW_K + v))
                        sp.dma_start(raw[v % 2][:, 0:src.shape[1] * src.shape[2]].rearrange(
                            "p (a c) -> p a c", a=src.shape[1]), src).then_inc(raw_in[v % 2], 16)

                    for j in range(2):
                        load_block(2 * j, wv_rows[1, hh * 2 + j].rearrange("p (a c) -> p a c", a=1))
                        load_block(2 * j + 1, next_head(j))
                        for c in range(CH):
                            m = 2 * j + c
                            sp.wait_ge(w_full, hf * (2 * KVH) + hh * 4 + (m + 2))
                            if m == 3 and not last:
                                load_packed(hh + 1)
                            sp.dma_start(w_dram[2 * m:2 * m + 2, :, bass.ds(hh * WC, WC)].rearrange("i p c -> p i c"),
                                         dense_w[m % 2]).then_inc(w_stored[m % 2], 16)
                            sp.wait_ge(kv_lo, hf * KVU + hh * 4 + (K0 + m + 1))
                            for part in range(2):
                                sp.dma_start(k_dram[hh * 2 + j, :, part, c * CT:(c + 1) * CT],
                                             kv_out[m][:, part, :].bitcast(F32)).then_inc(kv_stored[m], 16)

                with sp.Fori(0, KVH // 2 - 1) as hh:
                    key_heads(hh, lambda j: wk_heads[hh * 2 + (2 + j)])
                key_heads(KVH // 2 - 1, lambda j: wq_heads[j], last=True)

                def load_k(c, head):
                    sp.dma_start(k_parts[c].bitcast(F32),
                                 k_dram[head, :, :, c * CT:(c + 1) * CT]).then_inc(k_in[c], 16)

                def load_v(c, head):
                    sp.dma_start(v_parts[c].bitcast(F32),
                                 v_dram[head, :, c * TT // 2:(c + 1) * TT // 2]).then_inc(v_in[c], 16)

                def load_kv(c, head, units):
                    sp.wait_ge(ot_done, units)
                    load_k(c, head)
                    load_v(c, head)

                for k in range(V1, KVU):
                    if k == KVU - 1:
                        for s in range(4):
                            sp.wait_ge(kv_stored[s], hf * (KVU // 4 * 32) + (KVU if s == 0 else V1) // 4 * 32)
                            hold(sp)
                        load_k(0, 0)
                    store_kv(k)

                for s in range(4):
                    sp.wait_ge(kv_stored[s], (hf + 1) * (KVU // 4 * 32))
                for i in range(2):
                    sp.wait_ge(w_stored[i], (hf + 1) * (KVH * 16) + 16)
                load_v(0, 0)
                load_k(1, 0)
                load_v(1, 0)

                def pair(p, last=False):
                    for u in range(PU):
                        if last and u % 2:
                            continue
                        src = [wo_blocks[p, 0], None, wo_blocks[p, 1], None][u]
                        if u % 2:
                            src = wq_heads[2 * (p + 1) + u // 2]
                        i = RAW_B0 + (u // 2 if last else u)
                        slot = i % 2
                        sp.wait_ge(raw_split, hf * RAWS + p * PU + i)
                        dst = raw[slot][:, :].rearrange("p (a c) -> p a c", a=src.shape[1])
                        sp.dma_start(dst, src).then_inc(raw_in[slot], 16)
                        if not last and u == 3:
                            load_kv(0, (p + 1) // 2, hf * UNITS + p * PU + 2)
                            load_kv(1, (p + 1) // 2, hf * UNITS + p * PU + 4)

                with sp.Fori(0, PAIRS - 1) as p:
                    pair(p)
                pair(PAIRS - 1, last=True)
                for i in range(NH * RAW_V):
                    n, a = i // RAW_V, i % RAW_V
                    a = DENSE_ORDER[a] if n == 0 else a
                    load_raw(RAW_C0 + i, w_dram[2 * a:2 * a + 2, :, n * NW:(n + 1) * NW].rearrange("i p c -> p i c"))
                    if i == 1:
                        sp.wait_ge(q_rot, (hf + 1) * UNITS)
                        sp.dma_start(bias_rows, bias.rearrange("(a n) -> a n", a=1).broadcast_to([P, E])
                                     ).then_inc(bias_in, 16)
            for t in range(TT):
                sp.wait_ge(out_stored[t], (1 + HALVES) * 16)

        @block.tensor
        def _(pe):
            pe.wait_ge(ident_in, 16)
            with pe.Fori(0, HALVES) as hf:
                def weights_ready(blocks):
                    pe.wait_ge(raw_split, hf * RAWS + 1 + blocks)

                def transposes(r, tiles):
                    if r >= 2:
                        pe.wait_ge(tr_second, hf * TRS + (r - 1))
                    for i, tile in enumerate(tiles):
                        last = pe.transpose(ps[:, BK_T + r % 2, i * P:(i + 1) * P], tile, identity[:, :])
                    last.then_inc(tr_done, 1)

                def ctx_tile(t):
                    pe.wait_ge(ctx_in[t], hf * 16 + 16)
                    for g in range(2):
                        transposes(2 * t + g, [rows[:, t, (4 * g + i) * P:(4 * g + i + 1) * P] for i in range(4)])

                def norm_tile(r0, t, count):
                    source = x_normed if r0 == TR_X else normed
                    pe.wait_ge(ln_rows, hf * 2 * TT + count)
                    for g in range(2):
                        transposes(r0 + 2 * t + g, [source[t % 2][:, (4 * g + i) * P:(4 * g + i + 1) * P]
                                                    for i in range(4)])

                def kv_bank(k):
                    if k >= 2:
                        pe.wait_ge(kv_lo, hf * KVU + (k - 1))
                    return ps[:, BK_W + k % 2, :]

                def value_unit(k, t, weights=False):
                    def x_part(i):
                        if weights and i % 2 == 0:
                            weights_ready(i // 2 + 1)
                        return [act_v[:, part, i, t * P:(t + 1) * P] for part in range(2)]

                    products(pe, kv_bank(k), x_part,
                             lambda i: [wv_parts[:, i, part, :] for part in range(2)], KT).then_inc(kv_done, 1)

                def query_unit(v_unit, j, c, weights):
                    weights_ready(weights)
                    if v_unit is not None:
                        pe.wait_ge(q_rot, v_unit)
                    products(pe, ps[:, BK_Q, :],
                             lambda i: [wq_parts[:, j, i, part, :] for part in range(2)],
                             lambda i: [act_v[:, part, i, c * CT:(c + 1) * CT] for part in range(2)],
                             KT).then_inc(q_done, 1)

                ctx_tile(0)
                for t in range(TT):
                    pe.wait_ge(tr_second, hf * TRS + 2 * t + 2)
                    value_unit(t, t, weights=(t == 0))
                    if t == 0:
                        ctx_tile(1)
                    if t + 2 < TT:
                        ctx_tile(t + 2)
                    else:
                        pe.wait_ge(table_in, hf * (16 * TT) + 16 * TT)
                        for g in range(2 * (t + 2 - TT), 2 * (t + 2 - TT) + 2):
                            transposes(TR_CS + g, [gathered[:, 2 * g + i // 2, (i % 2) * P:(i % 2 + 1) * P]
                                                   for i in range(4)])
                weights_ready(RAW_K)
                hold(pe)
                with pe.Fori(0, KVH // 2) as hh:
                    for j in range(2):
                        for c in range(CH):
                            k = K0 + 2 * j + c
                            if c == 0:
                                weights_ready(hh * 4 + (RAW_K - 4 + 2 * j + 2))
                            pe.wait_ge(kv_lo, hf * KVU + hh * 4 + (k - 1))
                            products(pe, ps[:, BK_W + k % 2, :],
                                     lambda i: [wq_parts[:, j, i, part, :] for part in range(2)],
                                     lambda i: [act_v[:, part, i, c * CT:(c + 1) * CT] for part in range(2)],
                                     KT).then_inc(kv_done, 1)
                weights_ready(RAW_B0 - 1)
                for t in range(TT):
                    if t == TT - 2:
                        pe.wait_ge(tr_second, hf * TRS + TR_X + 2 * TT // CH)
                        query_unit(None, 0, 0, RAW_B0 - 2)
                    value_unit(V1 + t, t)
                    if t >= 1:
                        norm_tile(TR_X, t - 1, t)
                norm_tile(TR_X, TT - 1, TT)

                def output_tile(part, i, c, n, fresh=False):
                    if fresh and i < 2:
                        pe.wait_ge(kv_lo, (hf + 1) * KVU)
                    else:
                        pe.wait_ge(wo_added, part + (i - 1))
                    products(pe, ps[:, BK_W + i % 2, :],
                             lambda j: [o_parts[:, c, j, l, i * P:(i + 1) * P] for l in range(2)],
                             lambda j: [wo_parts[:, n, j, l, :] for l in range(2)], 2).then_inc(wo_done, 1)

                def unit(p, u, first=False, last=False):
                    j, c = u % 2, u // 2
                    at = hf * UNITS + p * PU + u
                    pe.wait_ge(q_lo, at + 1)
                    if j == 0:
                        pe.wait_ge(k_in[c], hf * (16 * PAIRS) + p * 16 + 16)
                    for b in range(CB):
                        if not (first and u == 0):
                            pe.wait_ge(s_masked, at * 2 - 1 + b)
                        for qt in range(2):
                            q0 = b * S + qt * P
                            last_mm = products(pe, ps[:, BK_S + b, qt * S:(qt + 1) * S],
                                               lambda i: [q_parts[:, l, q0:q0 + P] for l in range(2)],
                                               lambda i: [k_parts[c][:, l, b * S:(b + 1) * S] for l in range(2)], 1)
                        last_mm.then_inc(s_done, 1)
                    if not (last and u == PU - 1):
                        nu = (u + 1) % PU
                        nj = nu % 2
                        if u == PU - 1:
                            w = p * PU + (RAW_B0 + 2)
                        elif nj == 0:
                            w = p * PU + (RAW_B0 - 2)
                        else:
                            w = p * PU + RAW_B0
                        if first and u == 1:
                            pe.wait_ge(tr_second, hf * TRS + TR_X2)
                        query_unit(at + 1, nj, nu // 2, w)
                    part = hf * (PAIRS * WOS) + p * WOS + (u - 2) * 4
                    tiles = 0 if first and u < 2 else TT // CH
                    if u >= 2:
                        pe.wait_ge(ot_lo, at - u + 2)
                        w = 1 if u == 2 else 2 if last else 3
                        weights_ready(p * PU + (RAW_B0 + w))
                    elif not first:
                        pe.wait_ge(ot_lo, at - u)
                        weights_ready(p * PU + (RAW_B0 - 1))
                    late = CB if last and u == PU - 1 else 0
                    for i in range(max(tiles, CB)):
                        if i < tiles:
                            output_tile(part, i, 0 if u >= 2 else 1, u % 2, fresh=first and u == 2)
                        if 0 <= i - late < CB:
                            b = i - late
                            pe.wait_ge(p_ready, at * 2 + b + 1)
                            if not (first and u == 0):
                                pe.wait_ge(pt_lo, at * 2 + b - 1)
                            for kt in range(2):
                                for qt in range(2):
                                    last_t = pe.transpose(
                                        ps[:, BK_T + b, kt * S + qt * P:kt * S + (qt + 1) * P],
                                        probs_v[:, b, qt, kt * P:(kt + 1) * P], identity[:, :])
                            last_t.then_inc(pt_done, 1)
                    if j == 0:
                        pe.wait_ge(v_in[c], hf * (16 * PAIRS) + p * 16 + 16)
                    if not (first and u == 0):
                        pe.wait_ge(ot_lo, at)
                    for b in range(CB):
                        pe.wait_ge(pt_lo, at * 2 + b + 1)
                        last_mm = products(pe, ps[:, BK_O, b * S:(b + 1) * S],
                                           lambda kt: [v_parts[c][:, 2 * b + kt, l, :] for l in range(2)],
                                           lambda kt: [probs_t[:, b, kt, l, :] for l in range(2)], 2)
                    last_mm.then_inc(ot_done, 1)

                for u in range(PU):
                    unit(0, u, first=True)
                with pe.Fori(1, PAIRS - 1) as p:
                    for u in range(PU):
                        unit(p, u)
                for u in range(PU):
                    unit(PAIRS - 1, u, last=True)
                pe.wait_ge(ot_lo, (hf + 1) * UNITS)
                weights_ready(RAW_C0)
                for i in range(TT):
                    output_tile(hf * (PAIRS * WOS) + (PAIRS - 1) * WOS + TT + i // 4 * 4, i % 4, 1, i // 4)
                    if i in (5, 6):
                        norm_tile(TR_X2, i - 5, TT + i - 4)

                def dense_unit(k, n, t):
                    if t == 0:
                        weights_ready(RAW_C0 + (n + 1) * RAW_V)
                    if k >= 2:
                        pe.wait_ge(ffn_added, hf * (TT * NH) + (k - 1))
                    products(pe, ps[:, BK_W + k % 2, :],
                             lambda i: [act_v[:, part, i, t * P:(t + 1) * P] for part in range(2)],
                             lambda i: [w_parts[n][:, i, part, :] for part in range(2)], KT).then_inc(ffn_done, 1)

                pe.wait_ge(wo_added, (hf + 1) * (PAIRS * WOS))
                for t in range(TT):
                    pe.wait_ge(tr_second, hf * TRS + TR_X2 + 2 * t + 2)
                    dense_unit(t, 0, t)
                    if t + 2 < TT:
                        norm_tile(TR_X2, t + 2, TT + t + 3)
                for t in range(TT):
                    dense_unit(TT + t, 1, t)

        @block.scalar
        def _(act):
            with act.Fori(0, HALVES) as hf:
                def evacuate(r, cols, first=True):
                    act.wait_ge(tr_done, hf * TRS + r + 1)
                    act.activation(cols, ps[:, BK_T + r % 2, :].rearrange("p (k t) -> p k t", t=P),
                                   ACT.Copy).then_inc(tr_first, 1)

                def tile_hi(r0, t):
                    for g in range(2):
                        evacuate(r0 + 2 * t + g, act_v[:, 0, 4 * g:4 * g + 4, t * P:(t + 1) * P])

                def split_hi(i, dst, before=None, more=0, src_shape=None):
                    if before is not None:
                        act.wait_ge(*before)
                    if i < RAW_V:
                        act.wait_ge(raw_in[i], hf * ((RING if i < 2 else 1) * 16) + 16)
                        act.activation(dst, value_raw[i], ACT.Copy).then_inc(raw_hi, 1)
                        return
                    act.wait_ge(raw_in[i % 2], hf * (RING * 16) + more + (i // 2) * 16)
                    a, c = dst.shape[1:]
                    act.activation(dst, raw[i % 2][:, 0:a * c].rearrange("p (a c) -> p a c", a=a),
                                   ACT.Copy).then_inc(raw_hi, 1)

                def split_value(i, n, a, before=None):
                    split_hi(i, wv_parts[:, 2 * a:2 * a + 2, 0, :], before)

                def kv_unit_hi(k, more=0, rotated=False):
                    if k >= 4 or rotated:
                        act.wait_ge(kv_stored[k % 4], hf * (KVU // 4 * 32) + more * 32 + (k // 4) * 32)
                    if rotated:
                        act.wait_ge(k_sum, hf * (2 * KVH) + more * 4 + (k - K0 + 1))
                        act.activation(kv_out[k % 4][:, 0, :], rope_tmp[:, 0, :], ACT.Copy).then_inc(kv_hi, 1)
                    else:
                        act.wait_ge(kv_done, hf * KVU + (k + 1))
                        act.activation(kv_out[k % 4][:, 0, :], ps[:, BK_W + k % 2, :], ACT.Copy).then_inc(kv_hi, 1)

                def query_hi(count):
                    act.wait_ge(q_sum, count)
                    act.activation(q_parts[:, 0, :], rope_tmp[:, 0, :], ACT.Copy).then_inc(q_hi, 1)

                tile_hi(0, 0)
                act.wait_ge(half_open, hf + 1)
                for a in range(RAW_V):
                    split_value(a, 0, a)
                tile_hi(0, 1)
                for i in range(2):
                    split_hi(4 + i, wq_parts[:, i, :, 0, :])
                for t in range(TT):
                    kv_unit_hi(t)
                    if t + 2 < TT:
                        tile_hi(0, t + 2)
                        continue
                    for g in range(2 * (t + 2 - TT), 2 * (t + 2 - TT) + 2):
                        r = TR_CS + g
                        act.wait_ge(tr_done, hf * TRS + r + 1)
                        act.activation(
                            rope_cos[:, 2 * g * P:(2 * g + 2) * P].rearrange("p (t q) -> p t q", t=2),
                            ps[:, BK_T + r % 2, :].rearrange("p (t w q) -> p t w q", t=2, w=2)[:, :, 0, :],
                            ACT.Copy).then_inc(tr_first, 1)

                def root(which, tiles):
                    act.wait_ge(ln_var, hf * (1 + TT // 2) + which + 1)
                    act.activation(ln_tmp[:, 1, tiles], ln_tmp[:, 0, tiles], ACT.Sqrt).then_inc(ln_root, 1)

                with act.Fori(0, KVH // 2) as hh:
                    for j in range(2):
                        for c in range(CH):
                            kv_unit_hi(K0 + 2 * j + c, more=hh, rotated=True)
                            if c == 0:
                                split_hi(RAW_K + 2 * j, wv_parts[:, bass.ds(hh * 2 + j, 1), 0, :], more=hh * 32)
                        split_hi(RAW_K + 2 * j + 1, wq_parts[:, j, :, 0, :],
                                 (kv_done, hf * KVU + hh * 4 + (K0 + 2 * j + 2)), more=hh * 32)
                root(0, slice(0, TT))
                for t in range(TT):
                    if t == TT - 2:
                        query_hi(hf * UNITS + 1)
                    kv_unit_hi(V1 + t)
                    if t >= 1:
                        tile_hi(TR_X, t - 1)
                tile_hi(TR_X, TT - 1)

                def split_dense(n, i, before=None):
                    a = DENSE_ORDER[i] if n == 0 else i
                    split_hi(RAW_C0 + n * RAW_V + i, w_parts[n][:, 2 * a:2 * a + 2, 0, :], before)

                def unit(p, u, first=False, last=False):
                    j, c = u % 2, u // 2
                    at = hf * UNITS + p * PU + u
                    for b in range(CB):
                        act.wait_ge(max_ready, at * 2 + b + 1)
                        if not (first and u == 0):
                            act.wait_ge(pt_done, at * 2 + b - 1)
                        for qt in range(2):
                            i = 2 * b + qt
                            e = act.activation(probs_v[:, b, qt, :], score_v[:, 2 * c + b, qt, :], ACT.Exp,
                                               bias=neg_max[:, i:i + 1], scale=SCALE,
                                               accum_out=row_sum[:, i:i + 1])
                        e.then_inc(exp_done, 1)
                    for b in range(CB):
                        act.wait_ge(inv_ready, at * 2 + b + 1)
                        for qt in range(2):
                            i = 2 * b + qt
                            e = act.activation(probs_v[:, b, qt, :], probs_v[:, b, qt, :], ACT.Copy,
                                               scale=inv_sum[:, i:i + 1])
                        e.then_inc(p_ready, 1)

                    def split(v, dst, before):
                        i = RAW_B0 + v
                        split_hi(i, dst, before, more=p * 32)

                    if u == 2:
                        split(2 if not last else 1, wo_parts[:, 1, :, 0, :],
                              None if first else (wo_done, hf * (PAIRS * WOS) + p * WOS))
                    if u == 3 and not last:
                        split(3, wq_parts[:, 1, :, 0, :], (q_done, at + 1))
                    if u == 3 and last:
                        split_dense(0, 0, (ot_done, at - 1))
                    for b in range(CB):
                        act.wait_ge(pt_done, at * 2 + b + 1)
                        act.activation(probs_t[:, b, :, 0, :], ps[:, BK_T + b, :].rearrange("p (k q) -> p k q", k=2),
                                       ACT.Copy).then_inc(pt_hi, 1)
                    if not (last and u == PU - 1):
                        query_hi(at + 2)
                    if u == 0:
                        split(0, wo_parts[:, 0, :, 0, :],
                              None if first else (wo_done, hf * (PAIRS * WOS) + p * WOS - 4))
                    if u == 1 and not last:
                        split(1, wq_parts[:, 0, :, 0, :], (q_done, at + 2))
                    if u == 3 and last:
                        split_dense(0, 1, (q_done, (hf + 1) * UNITS))
                    act.wait_ge(ot_done, at + 1)
                    act.activation(o_parts[:, c, j, 0, :], ps[:, BK_O, :], ACT.Copy).then_inc(ot_hi, 1)

                for u in range(PU):
                    unit(0, u, first=True)
                with act.Fori(1, PAIRS - 1) as p:
                    for u in range(PU):
                        unit(p, u)
                for u in range(PU):
                    unit(PAIRS - 1, u, last=True)

                root(1, slice(0, 2))
                split_dense(0, 2)
                split_dense(0, 3)
                tile_hi(TR_X2, 0)
                tile_hi(TR_X2, 1)
                root(2, slice(2, 4))
                for t in range(TT):
                    if t + 2 < TT:
                        tile_hi(TR_X2, t + 2)
                    if t in (1, 3):
                        root(t // 2 + 3, slice(t + 3, t + 5))
                    if t < RAW_V:
                        split_dense(1, t, (wo_done, (hf + 1) * (PAIRS * WOS)))
                for t in range(TT):
                    act.wait_ge(ffn_added, hf * TT * NH + TT + t + 1)
                    act.dma_start(o_rows[hf, t], rows[:, t, :]).then_inc(out_stored[t], 16)

        @block.vector
        def _(dve):
            with dve.Fori(0, HALVES) as hf:
                def lo(dst, src, hi, sem_, value, done):
                    dve.wait_ge(sem_, value)
                    dve.tensor_tensor(dst, src, hi.bitcast(F32), ALU.subtract).then_inc(done, 1)

                def tile_lo(r0, t):
                    for g in range(2):
                        r = r0 + 2 * t + g
                        lo(act_v[:, 1, 4 * g:4 * g + 4, t * P:(t + 1) * P],
                           ps[:, BK_T + r % 2, :].rearrange("p (k t) -> p k t", t=P),
                           act_v[:, 0, 4 * g:4 * g + 4, t * P:(t + 1) * P],
                           tr_first, hf * TRS + r + 1, tr_second)

                def rotate(bank, t0, done):
                    dve.tensor_tensor(rope_tmp[:, 0, :], ps[:, bank, :], rope_cos[:, t0:t0 + CT], ALU.mult)
                    dve.tensor_tensor(rope_tmp[0:HD2, 1, :], ps[HD2:D, bank, :], rope_sin[HD2:D, t0:t0 + CT],
                                      ALU.mult)
                    dve.tensor_tensor(rope_tmp[HD2:D, 1, :], ps[0:HD2, bank, :], rope_sin[0:HD2, t0:t0 + CT],
                                      ALU.mult).then_inc(done, 1)

                def value_lo(k):
                    lo(kv_out[k % 4][:, 1, :], ps[:, BK_W + k % 2, :], kv_out[k % 4][:, 0, :],
                       kv_hi, hf * KVU + k + 1, kv_lo)

                def tile_stats(t):
                    for n in range(NH):
                        dve.bn_stats(stats[:, t, n, :], rows[:, t, n * NW:(n + 1) * NW]).then_inc(ln_chain, 1)

                def inverse_std(which, first, n):
                    before = hf * LN_LINKS + (LN_A + (which - 1) * LN_C if which else 0)
                    tiles = slice(first, first + n)
                    dve.wait_ge(ln_chain, before + 2 * n)
                    hold(dve)
                    for t in range(first, first + n):
                        dve.bn_aggr(mean_var[:, t, :], stats[:, t, :, :]).then_inc(ln_chain, 1)
                    dve.wait_ge(ln_chain, before + 3 * n)
                    dve.tensor_scalar(ln_tmp[:, 0, tiles], mean_var[:, tiles, 1], EPS, None,
                                      ALU.add).then_inc(ln_var, 1)
                    dve.wait_ge(ln_root, hf * (1 + TT // 2) + which + 1)
                    y, w, v = ln_tmp[:, 2, tiles], ln_tmp[:, 3, tiles], ln_tmp[:, 0, tiles]
                    steps = [
                        lambda: dve.reciprocal(y, ln_tmp[:, 1, tiles]),
                        lambda: dve.tensor_tensor(w, y, y, ALU.mult),
                        lambda: dve.tensor_tensor(w, w, v, ALU.mult),
                        lambda: dve.tensor_scalar(w, w, -0.5, 1.5, ALU.mult, ALU.add),
                        lambda: dve.tensor_tensor(inv_std[:, tiles], y, w, ALU.mult),
                    ]
                    for i, step in enumerate(steps):
                        step().then_inc(ln_chain, 1)
                        dve.wait_ge(ln_chain, before + 3 * n + i + 1)
                    hold(dve)

                def normalize(t, which):
                    if t >= 2:
                        dve.wait_ge(tr_done, hf * TRS + (TR_X, TR_X2)[which] + 2 * (t - 1))
                    dst = (x_normed, normed)[which][t % 2]
                    src = rows[:, t, :]
                    if which:
                        dst = dst.rearrange("p (j r) -> p j r", j=NIB)
                        src = src.rearrange("p (r j) -> p j r", j=NIB)
                    dve.tensor_scalar(dst, src, mean_var[:, t, 0:1], inv_std[:, t:t + 1],
                                      ALU.subtract, ALU.mult).then_inc(ln_rows, 1)

                def query_products(count, c, first=False):
                    dve.wait_ge(q_done, count)
                    if not first:
                        dve.wait_ge(q_lo, count - 1)
                    rotate(BK_Q, c * CT, q_rot)

                def query_lo(count):
                    lo(q_parts[:, 1, :], rope_tmp[:, 0, :], q_parts[:, 0, :], q_hi, count, q_lo)

                def x_stats(t):
                    dve.wait_ge(x_in[t], hf * 16 + 16)
                    tile_stats(t)

                tile_lo(0, 0)
                for i in range(RAW_V):
                    dve.wait_ge(raw_hi, hf * RAWS + i + 1)
                    dve.tensor_tensor(wv_parts[:, 2 * i:2 * i + 2, 1, :],
                                      value_raw[i],
                                      wv_parts[:, 2 * i:2 * i + 2, 0, :].bitcast(F32),
                                      ALU.subtract).then_inc(raw_split, 1)
                tile_lo(0, 1)
                dve.wait_ge(pos_in, hf * 16 + 16)
                dve.tensor_scalar(idx_neg[:, :], idx[:, :], 0, MAX_POS, ALU.is_lt, ALU.mult).then_inc(idx_step, 1)
                dve.wait_ge(idx_step, hf * 2 + 1)
                hold(dve)
                dve.tensor_tensor(idx[:, :], idx[:, :], idx_neg[:, :], ALU.add).then_inc(idx_step, 1)
                dve.wait_ge(idx_step, hf * 2 + 2)
                dve.tensor_scalar(idx[:, :], idx[:, :], 0, MAX_POS - 1, ALU.max, ALU.min).then_inc(idx_ready, 1)
                for t in range(TT):
                    value_lo(t)
                    if t + 2 < TT:
                        tile_lo(0, t + 2)
                    else:
                        for g in range(2 * (t + 2 - TT), 2 * (t + 2 - TT) + 2):
                            r = TR_CS + g
                            dve.wait_ge(tr_first, hf * TRS + r + 1)
                            dve.tensor_copy(
                                rope_sin[:, 2 * g * P:(2 * g + 2) * P].rearrange("p (t q) -> p t q", t=2),
                                ps[:, BK_T + r % 2, :].rearrange("p (t w q) -> p t w q", t=2, w=2)[:, :, 1, :],
                            ).then_inc(tr_second, 1)
                    if t in (3, 5):
                        c = (t - 3) // 2
                        dve.wait_ge(mask_in, (hf * CH + c + 1) * 16)
                        dve.tensor_scalar(mask_v[:, c * CB:(c + 1) * CB], mask_i, 0, None,
                                          ALU.not_equal).then_inc(mask_ready, 1)
                    for i in {2: [0], 3: [1], 4: [2], 5: [3], 6: [4, 5], 7: [6]}.get(t, []):
                        x_stats(i)
                dve.wait_ge(zero_words_in, 16)
                dve.wait_ge(tr_second, hf * TRS + TR_X)
                for i in range(NIB):
                    dve.tensor_scalar(zeros_i.rearrange("p (w i) -> p w i", i=NIB)[:, :, i], zero_words[:, :],
                                      BITS * i, 2 ** BITS - 1, ALU.logical_shift_right,
                                      ALU.bitwise_and).then_inc(z_step, 1)
                x_stats(TT - 1)
                dve.wait_ge(z_step, (hf + 1) * NIB)
                dve.wait_ge(mask_ready, (hf + 1) * CH)
                hold(dve)
                with dve.Fori(0, KVH // 2) as hh:
                    for j in range(2):
                        for c in range(CH):
                            k = K0 + 2 * j + c
                            n = 2 * j + c
                            dve.wait_ge(kv_done, hf * KVU + hh * 4 + k + 1)
                            dve.wait_ge(tr_second, hf * TRS + TR_X)
                            dve.wait_ge(kv_lo, hf * KVU + hh * 4 + k)
                            rotate(BK_W + k % 2, c * CT, k_rot)
                            w = dense_w[n % 2]
                            dve.wait_ge(w_stored[n % 2], hf * (KVH * 16) + hh * 32 + (n // 2 * 16 + 16))
                            if n == 0:
                                dve.wait_ge(packed_in, hf * (KVH // 2 * 16) + hh * 16 + 16)
                                dve.wait_ge(scale_in, hf * (KVH // 2 * 16) + hh * 16 + 16)
                            link = hf * (2 * KVH * 3) + hh * 12 + n * 3
                            for i in range(2):
                                dve.tensor_scalar(w[:, i, :].bitcast(I32), packed, BITS * (2 * n + i), 2 ** BITS - 1,
                                                  ALU.logical_shift_right, ALU.bitwise_and).then_inc(w_step, 1)
                            dve.wait_ge(w_step, link + 2)
                            dve.tensor_tensor(w, w.bitcast(I32),
                                              zeros_i[:, bass.ds(hh * WC, WC)].rearrange("p (a c) -> p a c", a=1)
                                              .broadcast_to([P, 2, WC]), ALU.subtract).then_inc(w_step, 1)
                            dve.wait_ge(w_step, link + 3)
                            dve.tensor_tensor(w, w, scale_rows.rearrange("p (a c) -> p a c", a=1)
                                              .broadcast_to([P, 2, WC]), ALU.mult).then_inc(w_full, 1)
                            lo(kv_out[k % 4][:, 1, :], rope_tmp[:, 0, :], kv_out[k % 4][:, 0, :],
                               kv_hi, hf * KVU + hh * 4 + k + 1, kv_lo)
                inverse_std(0, 0, TT)
                for i in range(2):
                    dve.wait_ge(w_stored[i], (hf + 1) * (KVH * 16) + 16)
                dve.wait_ge(kv_lo, hf * KVU + V1)
                for t in range(2):
                    normalize(t, 0)
                for t in range(TT):
                    if t == TT - 2:
                        query_products(hf * UNITS + 1, 0, first=True)
                        query_lo(hf * UNITS + 1)
                    value_lo(V1 + t)
                    if t >= 1:
                        tile_lo(TR_X, t - 1)
                        if t + 1 < TT:
                            normalize(t + 1, 0)
                tile_lo(TR_X, TT - 1)

                def add_output(k, t, n):
                    dve.wait_ge(wo_done, k + 1)
                    dst = rows[:, t, n * NW:(n + 1) * NW]
                    dve.tensor_tensor(dst, ps[:, BK_W + t % 2, :], dst, ALU.add).then_inc(wo_added, 1)

                def unit(p, u, first=False, last=False):
                    j, c = u % 2, u // 2
                    at = hf * UNITS + p * PU + u
                    for b in range(CB):
                        dve.wait_ge(s_done, at * 2 + b + 1)
                        if not (first and u == 0):
                            dve.wait_ge(exp_done, at * 2 + b - 1)
                        hold(dve)
                        dve.copy_predicated(score_v[:, 2 * c + b, :, :], mask_v[:, 2 * c + b, :, :],
                                            ps[:, BK_S + b, :].rearrange("p (q k) -> p q k", q=2)
                                            ).then_inc(s_masked, 1)
                    for b in range(CB):
                        dve.wait_ge(s_masked, at * 2 + b + 1)
                        dve.tensor_reduce(row_max[:, 2 * b:2 * b + 2], score_v[:, 2 * c + b, :, :], AX.X,
                                          ALU.max).then_inc(max_done, 1)
                    for b in range(CB):
                        dve.wait_ge(max_done, at * 2 + b + 1)
                        dve.tensor_scalar(neg_max[:, 2 * b:2 * b + 2], row_max[:, 2 * b:2 * b + 2], -SCALE, None,
                                          ALU.mult).then_inc(max_ready, 1)
                    for b in range(CB):
                        dve.wait_ge(exp_done, at * 2 + b + 1)
                        dve.reciprocal(inv_sum[:, 2 * b:2 * b + 2], row_sum[:, 2 * b:2 * b + 2]).then_inc(inv_ready, 1)
                    more = not (last and u == PU - 1)
                    if more:
                        query_products(at + 2, ((u + 1) % PU) // 2)
                    k0 = hf * (PAIRS * WOS) + p * WOS + (u - 2) * 4
                    t0, n = (0, u - 2) if u >= 2 else (TT // 2, u)
                    adds = 0 if first and u < 2 else 4
                    for i in range(4):
                        if i < adds:
                            add_output(k0 + i, t0 + i, n)
                        b = i - (0 if more else CB)
                        if 0 <= b < CB:
                            lo(probs_t[:, b, :, 1, :], ps[:, BK_T + b, :].rearrange("p (k q) -> p k q", k=2),
                               probs_t[:, b, :, 0, :], pt_hi, at * 2 + b + 1, pt_lo)
                        if i == CB and more:
                            query_lo(at + 2)
                    if last and u == PU - 1:
                        dve.wait_ge(wo_added, hf * (PAIRS * WOS) + (PAIRS - 1) * WOS + TT)
                        tile_stats(0)
                        tile_stats(1)
                    lo(o_parts[:, c, j, 1, :], ps[:, BK_O, :], o_parts[:, c, j, 0, :], ot_hi, at + 1, ot_lo)

                for u in range(PU):
                    if u % 2 == 0:
                        dve.wait_ge(fill_done, hf * CH + u // 2 + 1)
                    unit(0, u, first=True)
                with dve.Fori(1, PAIRS - 1) as p:
                    for u in range(PU):
                        unit(p, u)
                for u in range(PU):
                    unit(PAIRS - 1, u, last=True)
                dve.wait_ge(p_ready, (hf + 1) * (UNITS * CB))
                dve.wait_ge(pt_done, (hf + 1) * (UNITS * CB))
                dve.wait_ge(q_lo, (hf + 1) * UNITS)
                inverse_std(1, 0, 2)
                normalize(0, 1)
                normalize(1, 1)
                for i in range(TT):
                    add_output(hf * (PAIRS * WOS) + (PAIRS - 1) * WOS + TT + i, TT // 2 + i % 4, i // 4)
                    if i in (2, 4):
                        tile_stats(2 + (i - 2) // 2)
                    if i in (5, 6):
                        tile_lo(TR_X2, i - 5)
                dve.wait_ge(wo_added, (hf + 1) * (PAIRS * WOS))
                inverse_std(2, 2, 2)
                normalize(2, 1)
                normalize(3, 1)

                def add_dense(k, t, n):
                    dve.wait_ge(ffn_done, hf * (TT * NH) + k + 1)
                    if k == TT * NH - 1:
                        dve.sem_inc(half_open, 1)
                    if n == 0:
                        dve.wait_ge(biased, hf * TT + t + 1)
                    dst = rows[:, t, n * NW:(n + 1) * NW]
                    dve.tensor_tensor(dst, ps[:, BK_W + k % 2, :], dst, ALU.add).then_inc(ffn_added, 1)

                for t in range(TT):
                    if t + 2 < TT:
                        tile_lo(TR_X2, t + 2)
                    if t in (1, 3):
                        inverse_std(t // 2 + 3, t + 3, 2)
                        normalize(t + 3, 1)
                    add_dense(t, t, 0)
                    if t in (0, 2):
                        tile_stats(t + 4)
                        tile_stats(t + 5)
                    if t in (1, 3):
                        normalize(t + 4, 1)
                for t in range(TT):
                    add_dense(TT + t, t, 1)

        @block.gpsimd
        def _(pool):
            with pool.Fori(0, HALVES) as hf:
                def split_lo(i, dst, hi, more=0):
                    pool.wait_ge(raw_hi, hf * RAWS + more + i + 1)
                    a, c = dst.shape[1:]
                    pool.tensor_tensor(dst, raw[i % 2][:, 0:a * c].rearrange("p (a c) -> p a c", a=a),
                                       hi.bitcast(F32), ALU.subtract).then_inc(raw_split, 1)

                def rope_sum(wait, value, done):
                    pool.wait_ge(wait, value)
                    pool.tensor_tensor(rope_tmp[:, 0, :], rope_tmp[:, 0, :], rope_tmp[:, 1, :],
                                       ALU.add).then_inc(done, 1)

                pool.wait_ge(idx_ready, hf + 1)
                pool.wait_ge(half_open, hf + 1)
                hold(pool)
                for t in range(TT):
                    pool.indirect_dma_start(gathered[:, t, :], None, table,
                                            bass.IndirectOffsetOnAxis(ap=idx[:, t:t + 1], axis=0)
                                            ).then_inc(table_in, 16)
                pool.wait_ge(raw_split, hf * RAWS + 1 + RAW_V)
                for i in range(2):
                    split_lo(4 + i, wq_parts[:, i, :, 1, :], wq_parts[:, i, :, 0, :])
                with pool.Fori(0, KVH // 2) as hh:
                    for j in range(2):
                        for c in range(CH):
                            n = 2 * j + c
                            rope_sum(k_rot, hf * (2 * KVH) + hh * 4 + n + 1, k_sum)
                            if c == 0:
                                kt = bass.ds(hh * 2 + j, 1)
                                split_lo(RAW_K + 2 * j, wv_parts[:, kt, 1, :], wv_parts[:, kt, 0, :], more=hh * 4)
                        split_lo(RAW_K + 2 * j + 1, wq_parts[:, j, :, 1, :], wq_parts[:, j, :, 0, :], more=hh * 4)
                pool.wait_ge(w_full, (hf + 1) * (2 * KVH) + 1)
                hold(pool)
                pool.memset(scores[:, 0:CB * 2 * S], MASKED).then_inc(fill_done, 1)

                def split_dense(n, i):
                    a = DENSE_ORDER[i] if n == 0 else i
                    split_lo(RAW_C0 + n * RAW_V + i, w_parts[n][:, 2 * a:2 * a + 2, 1, :],
                             w_parts[n][:, 2 * a:2 * a + 2, 0, :])

                def unit(p, u, first=False, last=False):
                    at = hf * UNITS + p * PU + u

                    def split(v, dst, hi):
                        split_lo(RAW_B0 + v, dst, hi, more=p * PU)

                    if u == 2:
                        split(2 if not last else 1, wo_parts[:, 1, :, 1, :], wo_parts[:, 1, :, 0, :])
                    if u == 3 and not last:
                        split(3, wq_parts[:, 1, :, 1, :], wq_parts[:, 1, :, 0, :])
                    if u == 3 and last:
                        split_dense(0, 0)
                        split_dense(0, 1)
                    if not (last and u == PU - 1):
                        rope_sum(q_rot, at + 2, q_sum)
                    if u == 0:
                        split(0, wo_parts[:, 0, :, 1, :], wo_parts[:, 0, :, 0, :])
                    if u == 1 and not last:
                        split(1, wq_parts[:, 0, :, 1, :], wq_parts[:, 0, :, 0, :])

                rope_sum(q_rot, hf * UNITS + 1, q_sum)
                pool.wait_ge(tr_done, hf * TRS + TR_X2)
                hold(pool)
                pool.memset(scores[:, CB * 2 * S:], MASKED).then_inc(fill_done, 1)
                for u in range(PU):
                    unit(0, u, first=True)
                with pool.Fori(1, PAIRS - 1) as p:
                    for u in range(PU):
                        unit(p, u)
                for u in range(PU):
                    unit(PAIRS - 1, u, last=True)

                split_dense(0, 2)
                split_dense(0, 3)
                pool.wait_ge(bias_in, hf * 16 + 16)
                for t in range(TT):
                    pool.wait_ge(ln_rows, hf * 2 * TT + TT + t + 1)
                    pool.tensor_tensor(rows[:, t, :], rows[:, t, :], bias_rows, ALU.add).then_inc(biased, 1)
                    if t < RAW_V:
                        split_dense(1, t)


_INS = ["x", "ctx_4096", "pos_BxS2", "mask_BxSxS2_ik0", "L0_xattn_Wq", "L0_xattn_Wk", "L0_xattn_Wv",
        "L0_xattn_Wo", "L0_ffn_qweight", "L0_ffn_qzeros", "L0_ffn_scales", "L0_ffn_bias"]


def kernel(**inputs):
    import concourse.bacc as bacc
    from concourse.bass_utils import run_bass_kernel_spmd

    nc = bacc.Bacc("TRN2", target_bir_lowering=False, num_devices=1)
    arrays = {f"in_{name}": np.ascontiguousarray(inputs[name]) for name in _INS}
    arrays["in_rope_table"] = rope_table()
    arrays["in_identity"] = np.eye(P, dtype=np.float32)
    args = [nc.dram_tensor(name, a.shape, mybir.dt.from_np(a.dtype), kind="ExternalInput").ap()
            for name, a in arrays.items()]
    out = nc.dram_tensor("out", (B, S, E), F32, kind="ExternalOutput").ap()
    build(nc, *args, out)
    result = run_bass_kernel_spmd(nc, [arrays], core_ids=[0])
    return result.results[0]["out"]
```
